# Optimizing a Trainium2 kernel written in Bass

```python
import numpy as np
import jax
import jax.numpy as jnp

def _softmax(x, axis=-1):
    return jax.nn.softmax(x, axis=axis)

def _gelu(x):
    return jax.nn.gelu(x, approximate=True)

def _silu(x):
    return jax.nn.silu(x)

def _sigmoid(x):
    return jax.nn.sigmoid(x)

def _layernorm(x, axis=-1, eps=1e-05):
    m = jnp.mean(x, axis=axis, keepdims=True)
    v = jnp.var(x, axis=axis, keepdims=True)
    return (x - m) / jnp.sqrt(v + eps)

def _scatter_add(tgt, idx, src, axis=0):
    return tgt.at[idx].add(src)

def _segment_sum(src, seg, n):
    return jax.ops.segment_sum(src, seg, n)
kernel_name = 'mk_xattn_seq_d1_seqx_r4_12f0f5'

def setup_inputs(seed: int=0):
    np.random.seed(seed)
    _w = jnp.asarray

    def _rec_inputs():
        import jax
        import jax.numpy as jnp
        _rk = jax.random.key(seed)
        x = -0.0001951 + 1 * jax.random.normal(jax.random.fold_in(_rk, 1), (16, 112, 256), jnp.float32)
        _lenS = 112 - jax.random.randint(jax.random.fold_in(_rk, 7), (16,), 0, max(1, 112 // 4) + 1, jnp.int32)
        _lenS2 = 375 - jax.random.randint(jax.random.fold_in(_rk, 8), (16,), 0, max(1, 375 // 4) + 1, jnp.int32)
        _ctx_1024P = jax.random.normal(jax.random.fold_in(_rk, 11), (16, 16, 256), jnp.float32)
        _ctx_1024c = jax.random.dirichlet(jax.random.fold_in(_rk, 511), 0.3 * jnp.ones((16,), jnp.float32), (16, 375))
        _ctx_1024t = jnp.einsum('bsk,bkd->bsd', _ctx_1024c, _ctx_1024P)
        _ctx_1024t = _ctx_1024t * jax.lax.rsqrt(jnp.mean(jnp.square(_ctx_1024t)) + 1e-12) * 0.953939
        ctx_1024 = -4.82715e-05 + 0.999928 * (_ctx_1024t + 0.3 * jax.random.normal(jax.random.fold_in(_rk, 611), (16, 375, 256), jnp.float32))
        _validS = jnp.arange(112)[None, :] < _lenS[:, None]
        _validS2 = jnp.arange(375)[None, :] < _lenS2[:, None]
        _causal = jnp.tril(jnp.ones((112, 112), dtype=bool))
        mask_BxS_bf0 = jnp.logical_not(jnp.ones((16, 112), dtype=bool))
        return (x, ctx_1024, mask_BxS_bf0)
    x, ctx_1024, mask_BxS_bf0 = _rec_inputs()

    def _L0_xattn_setup():
        import jax, jax.numpy as jnp
        import numpy as np
        B, T, J, C, H = (16, 112, 112, 256, 16)
        HD = C // H
        NEG_INF = float('-inf')

        def _layernorm(x, g, b, eps=1e-05):
            mu = jnp.mean(x, axis=-1, keepdims=True)
            var = jnp.var(x, axis=-1, keepdims=True)
            return (x - mu) * jax.lax.rsqrt(var + eps) * g + b

        def _heads(x):
            Bv, S, _ = x.shape
            return x.reshape(Bv, S, H, HD).transpose(0, 2, 1, 3)

        def _merge(x):
            Bv, _, S, _ = x.shape
            return x.transpose(0, 2, 1, 3).reshape(Bv, S, C)

        def _forward(tgt, src, sa_wqkv, sa_wproj, sa_bproj, ed_wkv, ed_wq, ed_wproj, ed_bproj, ff_w1, ff_b1, ff_w2, ff_b2, ln1_g, ln1_b, ln2_g, ln2_b, ln3_g, ln3_b, tgt_padding_mask):
            scale = C ** (-0.5)
            x = _layernorm(tgt, ln1_g, ln1_b)
            qkv = x @ sa_wqkv
            q, k, v = (_heads(t) for t in jnp.split(qkv, 3, axis=-1))
            wei = jnp.einsum('bhtd,bhsd->bhts', q, k) * scale
            causal = jnp.tril(jnp.ones((T, T), bool))
            wei = jnp.where(causal[None, None], wei, NEG_INF)
            wei = jnp.where(tgt_padding_mask[:, None, None, :], NEG_INF, wei)
            wei = jax.nn.softmax(wei, axis=-1)
            sa_out = _merge(jnp.einsum('bhts,bhsd->bhtd', wei, v)) @ sa_wproj + sa_bproj
            result = tgt + sa_out
            xq = _layernorm(result, ln2_g, ln2_b)
            xs = _layernorm(src, ln2_g, ln2_b)
            kv = xs @ ed_wkv
            k2, v2 = (_heads(t) for t in jnp.split(kv, 2, axis=-1))
            q2 = _heads(xq @ ed_wq)
            wei2 = jnp.einsum('bhtd,bhjd->bhtj', q2, k2) * scale
            wei2 = jax.nn.softmax(wei2, axis=-1)
            ed_out = _merge(jnp.einsum('bhtj,bhjd->bhtd', wei2, v2)) @ ed_wproj + ed_bproj
            result = result + ed_out
            h = jax.nn.relu(_layernorm(tgt, ln3_g, ln3_b) @ ff_w1 + ff_b1)
            result = result + (h @ ff_w2 + ff_b2)
            return result
        key = jax.random.key(seed)
        ks = jax.random.split(key, 16)
        s = 0.02
        return {'tgt': jax.random.normal(ks[0], (B, T, C), jnp.float32), 'src': jax.random.normal(ks[1], (B, J, C), jnp.float32), 'sa_wqkv': jax.random.normal(ks[2], (C, 3 * C), jnp.float32) * s, 'sa_wproj': jax.random.normal(ks[3], (C, C), jnp.float32) * s, 'sa_bproj': jnp.zeros((C,), jnp.float32), 'ed_wkv': jax.random.normal(ks[4], (C, 2 * C), jnp.float32) * s, 'ed_wq': jax.random.normal(ks[5], (C, C), jnp.float32) * s, 'ed_wproj': jax.random.normal(ks[6], (C, C), jnp.float32) * s, 'ed_bproj': jnp.zeros((C,), jnp.float32), 'ff_w1': jax.random.normal(ks[7], (C, 4 * C), jnp.float32) * s, 'ff_b1': jnp.zeros((4 * C,), jnp.float32), 'ff_w2': jax.random.normal(ks[8], (4 * C, C), jnp.float32) * s, 'ff_b2': jnp.zeros((C,), jnp.float32), 'ln1_g': jnp.ones((C,), jnp.float32), 'ln1_b': jnp.zeros((C,), jnp.float32), 'ln2_g': jnp.ones((C,), jnp.float32), 'ln2_b': jnp.zeros((C,), jnp.float32), 'ln3_g': jnp.ones((C,), jnp.float32), 'ln3_b': jnp.zeros((C,), jnp.float32), 'tgt_padding_mask': jnp.zeros((B, T), bool)}
    _L0_xattn_all = _L0_xattn_setup()
    _L0_xattn_in = {k: v for k, v in _L0_xattn_all.items() if k in ('sa_wqkv', 'sa_wproj', 'sa_bproj', 'ed_wkv', 'ed_wq', 'ed_wproj', 'ed_bproj', 'ff_w1', 'ff_b1', 'ff_w2', 'ff_b2', 'ln1_g', 'ln1_b', 'ln2_g', 'ln2_b', 'ln3_g', 'ln3_b')}
    del _L0_xattn_all
    return {'x': x, 'ctx_1024': ctx_1024, 'mask_BxS_bf0': mask_BxS_bf0, 'L0_xattn_sa_wqkv': _L0_xattn_in['sa_wqkv'], 'L0_xattn_sa_wproj': _L0_xattn_in['sa_wproj'], 'L0_xattn_sa_bproj': _L0_xattn_in['sa_bproj'], 'L0_xattn_ed_wkv': _L0_xattn_in['ed_wkv'], 'L0_xattn_ed_wq': _L0_xattn_in['ed_wq'], 'L0_xattn_ed_wproj': _L0_xattn_in['ed_wproj'], 'L0_xattn_ed_bproj': _L0_xattn_in['ed_bproj'], 'L0_xattn_ff_w1': _L0_xattn_in['ff_w1'], 'L0_xattn_ff_b1': _L0_xattn_in['ff_b1'], 'L0_xattn_ff_w2': _L0_xattn_in['ff_w2'], 'L0_xattn_ff_b2': _L0_xattn_in['ff_b2'], 'L0_xattn_ln1_g': _L0_xattn_in['ln1_g'], 'L0_xattn_ln1_b': _L0_xattn_in['ln1_b'], 'L0_xattn_ln2_g': _L0_xattn_in['ln2_g'], 'L0_xattn_ln2_b': _L0_xattn_in['ln2_b'], 'L0_xattn_ln3_g': _L0_xattn_in['ln3_g'], 'L0_xattn_ln3_b': _L0_xattn_in['ln3_b']}

def reference(x, ctx_1024, mask_BxS_bf0, L0_xattn_sa_wqkv, L0_xattn_sa_wproj, L0_xattn_sa_bproj, L0_xattn_ed_wkv, L0_xattn_ed_wq, L0_xattn_ed_wproj, L0_xattn_ed_bproj, L0_xattn_ff_w1, L0_xattn_ff_b1, L0_xattn_ff_w2, L0_xattn_ff_b2, L0_xattn_ln1_g, L0_xattn_ln1_b, L0_xattn_ln2_g, L0_xattn_ln2_b, L0_xattn_ln3_g, L0_xattn_ln3_b):
    import jax
    import jax.numpy as jnp

    def _L0_xattn_ref(tgt, src, sa_wqkv, sa_wproj, sa_bproj, ed_wkv, ed_wq, ed_wproj, ed_bproj, ff_w1, ff_b1, ff_w2, ff_b2, ln1_g, ln1_b, ln2_g, ln2_b, ln3_g, ln3_b, tgt_padding_mask):
        import jax, jax.numpy as jnp
        import numpy as np
        B, T, J, C, H = (16, 112, 112, 256, 16)
        HD = C // H
        NEG_INF = float('-inf')

        def _layernorm(x, g, b, eps=1e-05):
            mu = jnp.mean(x, axis=-1, keepdims=True)
            var = jnp.var(x, axis=-1, keepdims=True)
            return (x - mu) * jax.lax.rsqrt(var + eps) * g + b

        def _heads(x):
            Bv, S, _ = x.shape
            return x.reshape(Bv, S, H, HD).transpose(0, 2, 1, 3)

        def _merge(x):
            Bv, _, S, _ = x.shape
            return x.transpose(0, 2, 1, 3).reshape(Bv, S, C)

        def _forward(tgt, src, sa_wqkv, sa_wproj, sa_bproj, ed_wkv, ed_wq, ed_wproj, ed_bproj, ff_w1, ff_b1, ff_w2, ff_b2, ln1_g, ln1_b, ln2_g, ln2_b, ln3_g, ln3_b, tgt_padding_mask):
            scale = C ** (-0.5)
            x = _layernorm(tgt, ln1_g, ln1_b)
            qkv = x @ sa_wqkv
            q, k, v = (_heads(t) for t in jnp.split(qkv, 3, axis=-1))
            wei = jnp.einsum('bhtd,bhsd->bhts', q, k) * scale
            causal = jnp.tril(jnp.ones((T, T), bool))
            wei = jnp.where(causal[None, None], wei, NEG_INF)
            wei = jnp.where(tgt_padding_mask[:, None, None, :], NEG_INF, wei)
            wei = jax.nn.softmax(wei, axis=-1)
            sa_out = _merge(jnp.einsum('bhts,bhsd->bhtd', wei, v)) @ sa_wproj + sa_bproj
            result = tgt + sa_out
            xq = _layernorm(result, ln2_g, ln2_b)
            xs = _layernorm(src, ln2_g, ln2_b)
            kv = xs @ ed_wkv
            k2, v2 = (_heads(t) for t in jnp.split(kv, 2, axis=-1))
            q2 = _heads(xq @ ed_wq)
            wei2 = jnp.einsum('bhtd,bhjd->bhtj', q2, k2) * scale
            wei2 = jax.nn.softmax(wei2, axis=-1)
            ed_out = _merge(jnp.einsum('bhtj,bhjd->bhtd', wei2, v2)) @ ed_wproj + ed_bproj
            result = result + ed_out
            h = jax.nn.relu(_layernorm(tgt, ln3_g, ln3_b) @ ff_w1 + ff_b1)
            result = result + (h @ ff_w2 + ff_b2)
            return result
        return _forward(tgt, src, sa_wqkv, sa_wproj, sa_bproj, ed_wkv, ed_wq, ed_wproj, ed_bproj, ff_w1, ff_b1, ff_w2, ff_b2, ln1_g, ln1_b, ln2_g, ln2_b, ln3_g, ln3_b, tgt_padding_mask)
    x = _L0_xattn_ref(x, ctx_1024, L0_xattn_sa_wqkv, L0_xattn_sa_wproj, L0_xattn_sa_bproj, L0_xattn_ed_wkv, L0_xattn_ed_wq, L0_xattn_ed_wproj, L0_xattn_ed_bproj, L0_xattn_ff_w1, L0_xattn_ff_b1, L0_xattn_ff_w2, L0_xattn_ff_b2, L0_xattn_ln1_g, L0_xattn_ln1_b, L0_xattn_ln2_g, L0_xattn_ln2_b, L0_xattn_ln3_g, L0_xattn_ln3_b, mask_BxS_bf0)
    return x

_drawn_inputs = setup_inputs


def setup_inputs(seed=0):
    import zlib

    import numpy as np

    out = dict(_drawn_inputs(seed))
    spreads = {'L0_xattn_sa_bproj': (0.0, 0.1),
     'L0_xattn_ed_bproj': (0.0, 0.1),
     'L0_xattn_ff_b1': (0.0, 0.1),
     'L0_xattn_ff_b2': (0.0, 0.1),
     'L0_xattn_ln1_g': (1.0, 0.6),
     'L0_xattn_ln1_b': (0.0, 0.781),
     'L0_xattn_ln2_g': (1.0, 0.6),
     'L0_xattn_ln2_b': (0.0, 0.8),
     'L0_xattn_ln3_g': (1.0, 0.587),
     'L0_xattn_ln3_b': (0.0, 0.533)}
    factors = {'L0_xattn_ed_wq': 40.021}
    for name, (base, spread) in spreads.items():
        noise = np.random.default_rng([zlib.crc32(name.encode()), seed]).standard_normal(out[name].shape)
        drawn = base * np.exp(spread * noise) if base else spread * noise
        out[name] = jnp.asarray(drawn.astype(out[name].dtype))
    for name, factor in factors.items():
        out[name] = (out[name] * factor).astype(out[name].dtype)
    return out
```

```python
from contextlib import ExitStack

import concourse.bass as bass
from concourse import mybir

F32 = mybir.dt.float32
F32R = mybir.dt.float32r
BF16 = mybir.dt.bfloat16
U8 = mybir.dt.uint8
U32 = mybir.dt.uint32
ALU = mybir.AluOpType
ACT = mybir.ActivationFunctionType
AX_X = mybir.AxisListType.X

P = 128
H = 16
BG = 4
EPS = 1e-5
MASKED = -1e30
SLOTS = 6
K_PART = (0, 1, 2, 0, 1, 0)
Q_PART = (0, 0, 0, 1, 1, 2)
MISC_BANKS, MAX_BANKS, SCORE_BANKS = 2, 2, 3
PROB_SLOTS = 6

MISC_READER = {"xT": "act", "qk1": "dve", "v1": "dve", "ff1": "act", "sT": "act", "k2": "dve", "v2": "dve",
               "o1": "dve", "o2": "act", "o3": "dve", "xq": "act", "q2": "dve"}


def group_steps(kt):
    nm = 2 * kt * 2
    s = [("mask",), ("resid",), ("ln1",)] + [("xT", k) for k in range(kt)] + [("split_x",)]
    s += [("qk1", m) for m in range(2 * kt)] + [("stack_q1",), ("stack_k1",)]
    s += [("v1", b) for b in range(BG)]

    def src_head(b):
        return [("ln_s", b)] + [("sT", b, k) for k in range(kt)] + [("split_s", b)]

    def src_k(b):
        return [("k2", b, m) for m in range(kt)] + [("stack_k2", b)]

    def src_v(b):
        return [("v2", b, c) for c in range(3)]

    s += src_head(0) + src_k(0) + src_v(0)
    s += [("ff1", m) for m in range(nm // 2)]
    s += [("max", 0, i) for i in range(4)]
    for u in range(BG):
        for g in range(4):
            s.append(("score", u, g, 0))
            if u + 1 < BG:
                s.append(("max", u + 1, g))
            if g:
                s.append(("pv", u, g - 1))
            if u:
                s += [[("o1", u - 1)], [("o2", u - 1)], [("o3", u - 1), ("ln2", u - 1)], [("xq", u - 1)]][g]
        s += [("pv", u, 3), ("ot", u)]
    u = BG - 1
    late = [("ff1", m) for m in range(nm // 2, nm)]
    q = len(late) // 4
    s += late[:q] + [("o1", u)] + late[q:2 * q] + [("o2", u)] + late[2 * q:3 * q] + [("o3", u), ("ln2", u)] + late[3 * q:]
    s += [("xq", u), ("split_xq",)] + src_head(1)
    s += [("q2", m) for m in range(kt)] + [("stack_q2",)] + src_k(1) + src_v(1)
    s += [("max", BG, i) for i in range(H)]
    for u in range(BG, 2 * BG):
        b = u - BG
        done = 0
        for g in range(4):
            for c in range(3):
                s.append(("score", u, g, c))
                want = -(-(3 * g + c + 1) * H // 12) if u + 1 < 2 * BG else 0
                s += [("max", u + 1, i) for i in range(done, want)]
                done = max(done, want)
                if g and c == 0:
                    s.append(("pv", u, g - 1))
            if b + 2 < BG:
                s += [src_head(b + 2), [], src_k(b + 2)[:-1], []][g]
        s += [("pv", u, 3), ("ot", u)]
        if b + 2 < BG:
            s += [("stack_k2", b + 2)] + src_v(b + 2)
        s += [("o1", u), ("ff2", u), ("o2", u), ("o3", u)]
    return s


class Order:

    def __init__(self, steps):
        self.steps = steps
        self.at = {s: i for i, s in enumerate(steps)}
        assert len(self.at) == len(steps)

    def before(self, step, *kinds):
        return sum(s[0] in kinds for s in self.steps[:self.at[step]])

    def total(self, *kinds):
        return sum(s[0] in kinds for s in self.steps)

    def misc(self):
        return [s for s in self.steps if s[0] in MISC_READER]


def layer_kernel(nc, x, src, maskT, wqkv, sa_wproj, sa_bproj, ed_wkv, ed_wq, ed_wproj, ed_bproj,
                 ff_w1, ff_b1, ff_w2, ff_b2, g1, b1, g2, b2, g3, b3, out):
    B, T, C = x.shape
    S = src.shape[1]
    KT = C // P
    HD = C // H
    FT = ff_w1.shape[1] // P
    NT = BG * T
    SC = S // 3
    VW = HD + 1
    GH = 4
    SCALE = float(C) ** -0.5
    GROUPS = B // BG
    assert NT <= 512 and SC <= P and SC * 3 == S and GH * T <= 512 and FT == 4 * KT and H * HD == C
    SP2 = S + S % 2

    steps = group_steps(KT)
    od = Order(steps)
    misc_steps = od.misc()
    misc_at = {s: i for i, s in enumerate(misc_steps)}
    NMISC = len(misc_steps)
    NREAD = {e: sum(MISC_READER[s[0]] == e for s in misc_steps) for e in ("act", "dve")}
    scores = [s for s in steps if s[0] == "score"]
    score_at = {s[1:]: i for i, s in enumerate(scores)}
    maxes = [s for s in steps if s[0] == "max"]
    max_at = {s[1:]: i for i, s in enumerate(maxes)}
    splits = [s for s in steps if s[0] in ("qk1", "k2", "q2")]
    split_at = {s: i for i, s in enumerate(splits)}
    lns = [s for s in steps if s[0] in ("ln1", "ln_s", "ln2")]
    ln_at = {s: i for i, s in enumerate(lns)}
    hilos = [s for s in steps if s[0] in ("split_x", "split_s", "split_xq")]
    hilo_at = {s: i for i, s in enumerate(hilos)}
    STACKS = ("stack_q1", "stack_k1", "stack_k2", "stack_q2")
    LAND = 16 * SLOTS
    NSCR = 16 * KT * od.total(*STACKS)
    NSC, NMX, NSP, NLN, NHL, NU = len(scores), len(maxes), len(splits), len(lns), len(hilos), 2 * BG

    def chunks(u):
        return 1 if u < BG else 3

    def misc_read_count(step):
        e = MISC_READER[step[0]]
        return sum(MISC_READER[s[0]] == e for s in misc_steps[:misc_at[step] + 1])

    with ExitStack() as ctx:
        def sb(name, shape, dt=F32):
            return ctx.enter_context(nc.sbuf_tensor(name, shape, dt))

        def ps(name, shape):
            return ctx.enter_context(nc.psum_tensor(name, shape, F32))

        def sem(name):
            return ctx.enter_context(nc.semaphore(name))

        wqk_hi = sb("wqk_hi", [P, KT, 2 * C], F32R)
        wqk_lo = sb("wqk_lo", [P, KT, 2 * C], F32R)
        wv1 = sb("wv1", [P, KT, C])
        wf1_hi = sb("wf1_hi", [P, KT, FT * P], F32R)
        wf1_lo = sb("wf1_lo", [P, KT, FT * P], F32R)
        wf2 = sb("wf2", [P, FT, C])
        wk2_hi = sb("wk2_hi", [P, KT, C], F32R)
        wk2_lo = sb("wk2_lo", [P, KT, C], F32R)
        wv2 = sb("wv2", [P, KT, C])
        wq2_hi = sb("wq2_hi", [P, KT, C], F32R)
        wq2_lo = sb("wq2_lo", [P, KT, C], F32R)
        wps = sb("wps", [P, KT, C])
        wpe = sb("wpe", [P, KT, C])
        gain = sb("gain", [P, 3, KT])
        offs = sb("offs", [P, 3, KT])
        bias1 = sb("bias1", [P, FT])
        NB = 2 * KT + KT + KT + FT
        bcol = sb("bcol", [P, NB])
        vb = sb("vb", [P, 2, KT])
        sab = sb("sab", [T, C])
        edb = sb("edb", [T, C])
        ident = sb("ident", [P, P])
        identb = sb("identb", [P, T], BF16)
        ones_t = sb("ones_t", [T, P], F32R)
        causal = sb("causal", [T, T])
        mhalf = sb("mhalf", [P, BG])
        epst = sb("epst", [P, BG])

        tb = sb("tb", [T, BG, C])
        xn = sb("xn", [T, BG, C])
        xT32 = sb("xT32", [P, KT, NT])
        xT_hi = sb("xT_hi", [P, KT, NT], F32R)
        xT_lo = sb("xT_lo", [P, KT, NT], F32R)
        hT = sb("hT", [P, FT, NT])
        qp = sb("qp", [P, KT, 3, NT], BF16)
        kp = sb("kp", [P, KT, 3, NT], BF16)
        rem = sb("rem", [P, 2, NT])
        qst = sb("qst", [P, H, NT], BF16)
        k1st = sb("k1st", [P, H, NT], BF16)
        k2st = [sb(f"k2st{i}", [P, H, S], BF16) for i in range(2)]
        v1 = sb("v1", [T, BG, H, VW])
        v2 = [sb(f"v2{i}", [SC, 3, H, VW]) for i in range(2)]
        xs = [sb(f"xs{i}", [SC, 3, C]) for i in range(2)]
        xsT32 = sb("xsT32", [P, KT, SP2])
        xsT_hi = sb("xsT_hi", [P, KT, SP2], F32R)
        xsT_lo = sb("xsT_lo", [P, KT, SP2], F32R)
        stats = sb("stats", [P, BG, 6])
        mv = sb("mv", [P, BG, 2])
        veps = sb("veps", [P, BG])
        rstd = sb("rstd", [P, BG])
        assert BG == 4
        mask8 = sb("mask8", [T, B], U8)
        pad = sb("pad", [T, B])
        padneg = sb("padneg", [T, BG])
        maskt = sb("maskt", [T, BG, T], BF16)
        negm = sb("negm", [T, 2, H])
        diag = sb("diag", [T, 2, H * T], F32R)
        prob = sb("prob", [P, PROB_SLOTS, GH * T])
        ot = sb("ot", [P, GH * T])
        rden = sb("rden", [T, H])
        att = sb("att", [T, H, HD])
        aT = sb("aT", [P, KT, T])
        ostage = sb("ostage", [T, 2, C])

        hflat = hT[:, :, :].rearrange("p f n -> p (f n)")
        vbt = rem[:, :, :].rearrange("p a n -> p (a n)")[:, 0:2 * KT * T].rearrange("p (a k t) -> p a k t", a=2, k=KT)
        edb2 = ostage[:, 0, :]
        pflat = prob[:, :, :].rearrange("p s n -> p (s n)")
        raw_f1 = hflat[:, 0:KT * FT * P].rearrange("p (k n) -> p k n", k=KT)
        raw_qkv = hflat[:, KT * FT * P:KT * FT * P + KT * 3 * C].rearrange("p (k n) -> p k n", k=KT)
        raw_kv = pflat[:, 0:KT * 2 * C].rearrange("p (k n) -> p k n", k=KT)
        raw_q2 = pflat[:, KT * 2 * C:KT * 3 * C].rearrange("p (k n) -> p k n", k=KT)

        misc = [ps(f"misc{i}", [P, 512]) for i in range(MISC_BANKS)]
        mxb = [ps(f"mxb{i}", [P, 512]) for i in range(MAX_BANKS)]
        scb = [ps(f"scb{i}", [P, 512]) for i in range(SCORE_BANKS)]
        pvb = ps("pvb", [P, 512])

        scr_q = nc.dram_tensor("scr_q", (KT, P, 3, NT), BF16).ap()
        scr_k1 = nc.dram_tensor("scr_k1", (KT, P, 3, NT), BF16).ap()
        scr_k2 = [nc.dram_tensor(f"scr_k2{i}", (KT, P, 3, S), BF16).ap() for i in range(2)]

        s_w = sem("weights_landed")
        s_vec = sem("vectors_landed")
        s_const = sem("constants_made")
        s_init = sem("vector_constants_made")
        s_mcol = sem("prologue_matmuls_done")
        s_fold = sem("gain_folded")
        s_fhi = sem("folded_hi_made")
        s_flo = sem("folded_lo_made")
        s_bcol = sem("bias_columns_made")
        s_vbt = sem("value_offsets_spread")
        s_rows = sem("bias_rows_made")
        s_xt = sem("tgt_landed")
        s_xs = [sem(f"src_landed{i}") for i in range(2)]
        s_pad = sem("pad_terms_made")
        s_mask = sem("mask_tile_made")
        s_bn = sem("row_stats_made")
        s_mv = sem("mean_var_made")
        s_ve = sem("var_plus_eps_made")
        s_rs = sem("rstd_made")
        s_norm = sem("rows_normalised")
        s_res = sem("residual_started")
        s_resb = sem("residual_has_cross_bias")
        s_full = sem("misc_bank_filled")
        s_read = {"act": sem("misc_bank_read_by_act"), "dve": sem("misc_bank_read_by_dve")}
        s_hi = sem("hi_made")
        s_lo = sem("lo_made")
        s_p1 = sem("part1_made")
        s_rem1 = sem("remainder_made")
        s_p2 = sem("part2_made")
        s_p3 = sem("part3_made")
        s_step = sem("wait_holder")
        s_step_dve = sem("wait_holder_dve")
        s_scr = sem("parts_in_scratch")
        s_qst = sem("q_stack_landed")
        s_k1st = sem("k1_stack_landed")
        s_k2st = [sem(f"k2_stack_landed{i}") for i in range(2)]
        s_mxf = sem("max_scores_made")
        s_mx = sem("max_made")
        s_dg = sem("diag_made")
        s_sc = sem("scores_made")
        s_ex = sem("probs_made")
        s_pv = sem("values_weighted")
        s_ot = sem("weighted_copied")
        s_rd = sem("reciprocals_made")
        s_out = [sem(f"output_stored{i}") for i in range(2)]

        ahead_pe = [(s, 1) for s in (s_full, s_sc, s_pv)]
        ahead_act = [(s_read["act"], 1), (s_ex, 1), (s_ot, 1)]
        ahead_dve = [(s_read["dve"], 1), (s_lo, 1), (s_mx, 1)]
        ahead_pool = [(s_dg, 1)]
        ahead_sp = [(s_scr, 16), (s_out[0], 16), (s_out[1], 16)]
        start_of = {id(s): n for s, n in ahead_pe + ahead_act + ahead_dve + ahead_pool + ahead_sp}

        def count_ahead(eng, sems):
            for s, n in sems:
                eng.sem_inc(s, n)

        def up(eng, s, G, per, k):
            assert k > 0 or id(s) in start_of
            eng.wait_ge(s, G * per + max(k, 0) + start_of.get(id(s), 0))

        def misc_bank(step):
            return misc[misc_at[step] % MISC_BANKS]

        def wait_misc_free(pe, G, step):
            n = misc_at[step] - MISC_BANKS
            prev = misc_steps[n]
            up(pe, s_read[MISC_READER[prev[0]]], G, NREAD[MISC_READER[prev[0]]],
               misc_read_count(prev) if n >= 0 else 0)

        def wait_misc_full(eng, G, step):
            up(eng, s_full, G, NMISC, misc_at[step] + 1)

        block = ctx.enter_context(nc.Block())

        @block.sync
        def _(sp):
            count_ahead(sp, ahead_sp)
            ctx.enter_context(nc.allow_non_contiguous_dma(reason="vectors by model dimension, mask bytes"))

            def w(dst, source):
                sp.dma_start(dst, source.rearrange("(k p) n -> p k n", p=P)).then_inc(s_w, 16)

            def v(dst, source):
                sp.dma_start(dst, source.rearrange("(k p) -> p k", p=P)).then_inc(s_vec, 16)

            for i, (g, b) in enumerate(((g1, b1), (g2, b2), (g3, b3))):
                v(gain[:, i, :], g)
                v(offs[:, i, :], b)
            v(bias1[:, :], ff_b1)
            sp.dma_start(mask8[:, :].bitcast(U32), maskT).then_inc(s_vec, 16)
            w(raw_qkv, wqkv)
            w(raw_kv, ed_wkv)
            w(raw_q2, ed_wq)
            w(raw_f1, ff_w1)
            w(wps[:, :, :], sa_wproj)
            w(wpe[:, :, :], ed_wproj)
            w(wf2[:, :, :], ff_w2)
            for dst, vec in ((sab[:, :], sa_bproj), (edb[:, :], ed_bproj), (edb2, ff_b2)):
                sp.dma_start(dst, vec.rearrange("(a n) -> a n", a=1).broadcast_to([T, C])).then_inc(s_vec, 16)

            def stack(G, s, parts, last_split, scr, n, dst, part_of, landed, free=None):
                for m in range(KT):
                    up(sp, s_p3, G, NSP, split_at[last_split] + 2 + m - KT)
                    sp.dma_start(scr[m, :, :, 0:n], parts[:, m, :, 0:n]).then_inc(s_scr, 16)
                up(sp, s_scr, G, NSCR, 16 * KT * (1 + od.before(s, *STACKS)))
                if free is not None:
                    sp.sem_inc(s_step, 1)
                    up(sp, s_sc, G, NSC, free)
                for slot in range(SLOTS):
                    sp.dma_start(dst[HD * slot:HD * (slot + 1), :, 0:n],
                                 scr[:, :, part_of[slot], 0:n].rearrange("k (h d) t -> d (k h) t", d=HD)).then_inc(landed, 16)

            with sp.Fori(0, GROUPS) as G:
                for s in steps:
                    kind = s[0]
                    if kind == "mask":
                        up(sp, s_full, G, NMISC, 0)
                        sp.dma_start(xn[:, :, :], x[bass.ds(G * BG, BG), :, :].rearrange("b t c -> t b c")).then_inc(s_xt, 16)
                        for b in range(2):
                            sp.dma_start(xs[b][:, :, :], src[bass.ds(G * BG + b, 1), :, :].rearrange("a (c s) n -> s (a c) n", c=3)).then_inc(s_xs[b], 16)
                    elif kind == "stack_q1":
                        stack(G, s, qp, ("qk1", KT - 1), scr_q, NT, qst, Q_PART, s_qst)
                    elif kind == "stack_k1":
                        stack(G, s, kp, ("qk1", 2 * KT - 1), scr_k1, NT, k1st, K_PART, s_k1st)
                    elif kind == "stack_q2":
                        stack(G, s, qp, ("q2", KT - 1), scr_q, NT, qst, Q_PART, s_qst)
                    elif kind == "stack_k2":
                        b = s[1]
                        stack(G, s, kp, ("k2", b, KT - 1), scr_k2[b % 2], S, k2st[b % 2], K_PART, s_k2st[b % 2],
                              score_at[BG + b - 2, 3, 2] + 1 if b >= 2 else None)
                        if b + 2 < BG:
                            up(sp, s_full, G, NMISC, misc_at["sT", b, KT - 1] + 1)
                            sp.dma_start(xs[b % 2][:, :, :], src[bass.ds(G * BG + b + 2, 1), :, :].rearrange("a (c s) n -> s (a c) n", c=3)).then_inc(s_xs[b % 2], 16)
                    elif kind == "o3" and s[1] >= BG:
                        b = s[1] - BG
                        up(sp, s_read["dve"], G, NREAD["dve"], misc_read_count(s))
                        sp.dma_start(out[bass.ds(G * BG + b, 1), :, :].rearrange("a t c -> t (a c)"), ostage[:, b % 2, :]).then_inc(s_out[b % 2], 16)
            for i in range(2):
                sp.wait_ge(s_out[i], 16 * B // 2 + 16)

        @block.gpsimd
        def _(pool):
            count_ahead(pool, ahead_pool)
            nc.gpsimd.memset(ident[:, :], 0.0).then_inc(s_const, 1)
            nc.gpsimd.memset(causal[:, :], 0.0).then_inc(s_const, 1)
            nc.gpsimd.memset(mhalf[:, :], -0.5).then_inc(s_const, 1)
            nc.gpsimd.memset(epst[:, :], EPS).then_inc(s_const, 1)
            pool.wait_ge(s_const, 4)
            nc.gpsimd.affine_select(out=ident[:, :], in_=ident[:, :], compare_op=ALU.not_equal, fill=1.0,
                                    base=0, pattern=[[-1, P]], channel_multiplier=1).then_inc(s_const, 1)
            nc.gpsimd.affine_select(out=causal[:, :], in_=causal[:, :], compare_op=ALU.is_ge, fill=MASKED,
                                    base=0, pattern=[[1, T]], channel_multiplier=-1).then_inc(s_const, 1)
            pool.wait_ge(s_const, 6)
            pool.wait_ge(s_rows, 2)
            with pool.Fori(0, GROUPS) as G:
                for s in steps:
                    kind = s[0]
                    if kind in ("ln1", "ln_s", "ln2"):
                        n, rows = {"ln1": (BG, T), "ln_s": (3, SC), "ln2": (1, T)}[kind]
                        up(pool, s_mv, G, NLN, ln_at[s] + 1)
                        nc.gpsimd.tensor_tensor(veps[0:rows, 0:n], mv[0:rows, 0:n, 1], epst[0:rows, 0:n], ALU.add).then_inc(s_ve, 1)
                        up(pool, s_ve, G, NLN, ln_at[s] + 1)
                        nc.gpsimd.tensor_tensor(rstd[0:rows, 0:n], veps[0:rows, 0:n], mhalf[0:rows, 0:n], ALU.pow).then_inc(s_rs, 1)
                        if kind == "ln2":
                            b = s[1]
                            up(pool, s_norm, G, NLN, ln_at[s] + 1)
                            nc.gpsimd.tensor_tensor(tb[:, b, :], tb[:, b, :], edb[:, :], ALU.add).then_inc(s_resb, 1)
                    elif kind == "resid":
                        up(pool, s_xt, G, 16, 16)
                        up(pool, s_read["dve"], G, NREAD["dve"], 0)
                        nc.gpsimd.tensor_tensor(tb[:, :, :], xn[:, :, :], sab[:, :].unsqueeze(1).broadcast_to([T, BG, C]), ALU.add).then_inc(s_res, 1)
                    elif kind == "max":
                        u, i = s[1], s[2]
                        last = i if u < BG else i // GH
                        if u >= BG and i % GH != GH - 1:
                            continue
                        g = last
                        up(pool, s_mx, G, NMX, max_at[u, i] + 1)
                        if g == 0 and u >= 2:
                            up(pool, s_sc, G, NSC, score_at[u - 2, 3, chunks(u - 2) - 1] + 1)
                        elif g == 0:
                            up(pool, s_sc, G, NSC, 0)
                        nc.gpsimd.tensor_tensor(diag[:, u % 2, g * GH * T:(g + 1) * GH * T].rearrange("p (h t) -> p h t", h=GH),
                                                ident[0:T, 0:T].unsqueeze(1).broadcast_to([T, GH, T]),
                                                negm[:, u % 2, g * GH:(g + 1) * GH].unsqueeze(2).broadcast_to([T, GH, T]),
                                                ALU.mult).then_inc(s_dg, 1)

        @block.scalar
        def _(act):
            count_ahead(act, ahead_act)
            act.wait_ge(s_rows, 2)
            with act.Fori(0, GROUPS) as G:
                for s in steps:
                    kind = s[0]
                    if kind in ("xT", "xq", "sT", "o2", "ff1"):
                        wait_misc_full(act, G, s)
                    bank = misc_bank(s) if kind in MISC_READER else None
                    if kind == "xT":
                        k = s[1]
                        up(act, s_lo, G, NHL, 0)
                        up(act, s_full, G, NMISC, 0)
                        nc.scalar.activation(xT32[:, k, :], bank[:, 0:NT], ACT.Copy).then_inc(s_read["act"], 1)
                    elif kind == "xq":
                        b = s[1]
                        up(act, s_full, G, NMISC, misc_at["v1", BG - 1] + 1)
                        up(act, s_lo, G, NHL, hilo_at["split_x",] + 1)
                        nc.scalar.activation(xT32[:, :, b * T:(b + 1) * T], bank[:, 0:KT * T].rearrange("p (k t) -> p k t", k=KT), ACT.Copy).then_inc(s_read["act"], 1)
                    elif kind == "sT":
                        b, k = s[1:]
                        if b:
                            up(act, s_lo, G, NHL, hilo_at["split_s", b - 1] + 1)
                            up(act, s_full, G, NMISC, misc_at["v2", b - 1, 2] + 1)
                        else:
                            up(act, s_lo, G, NHL, 0)
                            up(act, s_full, G, NMISC, 0)
                        nc.scalar.activation(xsT32[:, k, 0:S], bank[:, 0:S], ACT.Copy).then_inc(s_read["act"], 1)
                    elif kind == "ff1":
                        m = s[1]
                        up(act, s_full, G, NMISC, 0)
                        nc.scalar.activation(hT[:, m, :], bank[:, 0:NT], ACT.Relu, bias=bcol[:, 4 * KT + m:4 * KT + m + 1]).then_inc(s_read["act"], 1)
                    elif kind == "o2":
                        u = s[1]
                        up(act, s_full, G, NMISC, misc_at["o3", u - 1] + 1 if u else 0)
                        nc.scalar.activation(aT[:, :, :], bank[:, 0:KT * T].rearrange("p (k t) -> p k t", k=KT), ACT.Copy).then_inc(s_read["act"], 1)
                    elif kind == "score":
                        u, g, c = s[1:]
                        n = score_at[u, g, c]
                        rows = T if u < BG else SC
                        up(act, s_sc, G, NSC, n + 1)
                        if n >= PROB_SLOTS:
                            ou, og, _ = scores[n - PROB_SLOTS][1:]
                            up(act, s_pv, G, 4 * NU, 4 * ou + og + 1)
                        else:
                            up(act, s_pv, G, 4 * NU, 0)
                        nc.scalar.activation(prob[0:rows, n % PROB_SLOTS, :], scb[n % SCORE_BANKS][0:rows, 0:GH * T], ACT.Exp,
                                             scale=SCALE).then_inc(s_ex, 1)
                    elif kind == "ot":
                        u = s[1]
                        up(act, s_pv, G, 4 * NU, 4 * u + 4)
                        up(act, s_full, G, NMISC, misc_at["o1", u - 1] + 1 if u else 0)
                        nc.scalar.activation(ot[:, :], pvb[:, 0:GH * T], ACT.Copy).then_inc(s_ot, 1)

        @block.vector
        def _(dve):
            count_ahead(dve, ahead_dve)
            V = nc.vector
            V.memset(ones_t[:, :].bitcast(F32), 1.0).then_inc(s_init, 1)
            V.memset(pvb[:, :], 0.0).then_inc(s_init, 1)
            V.memset(v1[:, :, :, HD:VW], 1.0).then_inc(s_init, 1)
            for i in range(2):
                V.memset(v2[i][:, :, :, HD:VW], 1.0).then_inc(s_init, 1)
                V.memset(k2st[i][HD * SLOTS:P, :, :], 0.0).then_inc(s_init, 1)
            V.memset(qst[HD * SLOTS:P, :, :], 0.0).then_inc(s_init, 1)
            V.memset(k1st[HD * SLOTS:P, :, :], 0.0).then_inc(s_init, 1)
            V.memset(xsT32[:, :, :], 0.0).then_inc(s_init, 1)
            dve.wait_ge(s_const, 6)
            V.tensor_copy(identb[0:T, :], ident[0:T, 0:T]).then_inc(s_init, 1)
            dve.wait_ge(s_vec, 176)
            dve.wait_ge(s_w, 7 * 16)
            V.tensor_tensor(edb[:, :], edb[:, :], edb2, ALU.add).then_inc(s_init, 1)
            V.tensor_scalar(pad[:, :], mask8[:, :], MASKED, None, ALU.mult).then_inc(s_init, 1)
            for k in range(KT):
                V.tensor_scalar(wv1[:, k, :], raw_qkv[:, k, 2 * C:3 * C], gain[:, 0, k:k + 1], None, ALU.mult).then_inc(s_init, 1)
                V.tensor_scalar(wv2[:, k, :], raw_kv[:, k, C:2 * C], gain[:, 1, k:k + 1], None, ALU.mult).then_inc(s_init, 1)
            dve.wait_ge(s_mcol, 1)
            folds = ((raw_qkv[:, :, 0:2 * C], 0, wqk_hi, wqk_lo), (raw_kv[:, :, 0:C], 1, wk2_hi, wk2_lo),
                     (raw_q2, 1, wq2_hi, wq2_lo), (raw_f1, 2, wf1_hi, wf1_lo))
            for n, (raw, i, hi, lo) in enumerate(folds):
                for k in range(KT):
                    V.tensor_scalar(raw[:, k, :], raw[:, k, :], gain[:, i, k:k + 1], None, ALU.mult).then_inc(s_fold, 1)
                dve.wait_ge(s_fold, KT * (n + 1))
                V.tensor_copy(hi[:, :, :], raw).then_inc(s_fhi, 1)
                dve.wait_ge(s_fhi, n + 1)
                V.tensor_tensor(lo[:, :, :], raw, hi[:, :, :].bitcast(F32), ALU.subtract).then_inc(s_flo, 1)
            V.tensor_copy(bcol[:, 0:4 * KT], misc[0][:, 0:4 * KT]).then_inc(s_bcol, 1)
            V.tensor_tensor(bcol[:, 4 * KT:NB], misc[0][:, 4 * KT:NB], bias1[:, :], ALU.add).then_inc(s_bcol, 1)
            V.tensor_copy(vb[:, :, :], misc[0][:, NB:NB + 2 * KT].rearrange("p (a k) -> p a k", a=2)).then_inc(s_bcol, 1)
            dve.wait_ge(s_bcol, 3)
            V.tensor_copy(vbt[:, :, :, :], vb[:, :, :].unsqueeze(3).broadcast_to([P, 2, KT, T])).then_inc(s_vbt, 1)
            dve.wait_ge(s_mcol, 2)
            dve.wait_ge(s_init, 13)
            V.tensor_tensor(sab[:, :], misc[1][0:T, 0:C], sab[:, :], ALU.add).then_inc(s_rows, 1)
            V.tensor_tensor(edb[:, :], misc[1][0:T, C:2 * C], edb[:, :], ALU.add).then_inc(s_rows, 1)

            def norm(G, s, src_of, dst_of, n, rows, first):
                for j in range(n):
                    i = V.bn_stats(stats[0:rows, j, :], src_of(j))
                i.then_inc(s_bn, 1)
                up(dve, s_bn, G, NLN, ln_at[s] + 1)
                dve.sem_inc(s_step_dve, 1)
                for j in range(n):
                    i = V.bn_aggr(mv[0:rows, j, :], stats[0:rows, j, :])
                i.then_inc(s_mv, 1)
                first()
                up(dve, s_rs, G, NLN, ln_at[s] + 1)
                for j in range(n):
                    i = V.tensor_scalar(dst_of(j), src_of(j), mv[0:rows, j, 0:1], rstd[0:rows, j:j + 1], ALU.subtract, ALU.mult)
                i.then_inc(s_norm, 1)

            def hilo(G, s, x32, hi, lo):
                V.tensor_copy(hi, x32).then_inc(s_hi, 1)
                up(dve, s_hi, G, NHL, hilo_at[s] + 1)
                V.tensor_tensor(lo, x32, hi.bitcast(F32), ALU.subtract).then_inc(s_lo, 1)

            def split3(G, s, bank, n, bias, parts, r):
                i = split_at[s] + 1
                V.tensor_scalar(parts[:, 0, 0:n], bank[:, 0:n], bias, None, ALU.add).then_inc(s_p1, 1)
                up(dve, s_p1, G, NSP, i)
                V.scalar_tensor_tensor(r[:, 0:n], bank[:, 0:n], bias, parts[:, 0, 0:n], ALU.add, ALU.subtract).then_inc(s_read["dve"], 1)
                up(dve, s_read["dve"], G, NREAD["dve"], misc_read_count(s))
                V.tensor_copy(parts[:, 1, 0:n], r[:, 0:n]).then_inc(s_p2, 1)
                up(dve, s_p2, G, NSP, i)
                V.tensor_tensor(parts[:, 2, 0:n], r[:, 0:n], parts[:, 1, 0:n], ALU.subtract).then_inc(s_p3, 1)

            with dve.Fori(0, GROUPS) as G:
                for s in steps:
                    kind = s[0]
                    bank = misc_bank(s) if kind in MISC_READER else None
                    if MISC_READER.get(kind) == "dve":
                        wait_misc_full(dve, G, s)
                    if kind == "mask":
                        V.tensor_copy(padneg[:, :], pad[:, bass.ds(G * BG, BG)]).then_inc(s_pad, 1)
                        up(dve, s_pad, G, 1, 1)
                        up(dve, s_sc, G, NSC, 0)
                        for b in range(BG):
                            i = V.tensor_scalar(maskt[:, b, :], causal[:, :], padneg[:, b:b + 1], None, ALU.add)
                        i.then_inc(s_mask, 1)
                    elif kind == "ln1":
                        up(dve, s_xt, G, 16, 16)
                        norm(G, s, lambda j: xn[:, j, :], lambda j: xn[:, j, :], BG, T,
                             lambda: up(dve, s_res, G, 1, 1))
                    elif kind == "ln_s":
                        b = s[1]
                        up(dve, s_xs[b % 2], G, 32, 16 * (b // 2 + 1))
                        norm(G, s, lambda j: xs[b % 2][:, j, :], lambda j: xs[b % 2][:, j, :], 3, SC, lambda: None)
                    elif kind == "ln2":
                        b = s[1]
                        up(dve, s_read["dve"], G, NREAD["dve"], misc_read_count(("o3", b)))
                        norm(G, s, lambda j: tb[:, b, :], lambda j: xn[:, b, :], 1, T,
                             lambda: up(dve, s_full, G, NMISC, misc_at["xT", KT - 1] + 1))
                    elif kind == "split_x":
                        up(dve, s_read["act"], G, NREAD["act"], misc_read_count(("xT", KT - 1)))
                        up(dve, s_full, G, NMISC, 0)
                        hilo(G, s, xT32[:, :, :], xT_hi[:, :, :], xT_lo[:, :, :])
                    elif kind == "split_s":
                        b = s[1]
                        up(dve, s_read["act"], G, NREAD["act"], misc_read_count(("sT", b, KT - 1)))
                        up(dve, s_full, G, NMISC, misc_at["k2", b - 1, KT - 1] + 1 if b else 0)
                        hilo(G, s, xsT32[:, :, :], xsT_hi[:, :, :], xsT_lo[:, :, :])
                    elif kind == "split_xq":
                        up(dve, s_read["act"], G, NREAD["act"], misc_read_count(("xq", BG - 1)))
                        up(dve, s_full, G, NMISC, misc_at["ff1", FT - 1] + 1)
                        hilo(G, s, xT32[:, :, :], xT_hi[:, :, :], xT_lo[:, :, :])
                    elif kind in ("qk1", "q2", "k2"):
                        if kind == "qk1":
                            m = s[1]
                            parts, n, col = (qp, kp)[m // KT][:, m % KT], NT, m
                            up(dve, s_scr, G, NSCR, 0)
                        elif kind == "q2":
                            m = s[1]
                            parts, n, col = qp[:, m], NT, 3 * KT + m
                            up(dve, s_scr, G, NSCR, 16 * KT)
                        else:
                            b, m = s[1:]
                            parts, n, col = kp[:, m], S, 2 * KT + m
                            up(dve, s_scr, G, NSCR, 16 * KT * od.before(("stack_k2", b), *STACKS))
                        split3(G, s, bank, n, bcol[:, col:col + 1], parts, rem[:, split_at[s] % 2])
                    elif kind == "v1":
                        b = s[1]
                        up(dve, s_pv, G, 4 * NU, 0)
                        V.tensor_copy(v1[:, b, :, 0:HD], bank[0:T, 0:C].rearrange("p (h d) -> p h d", h=H)).then_inc(s_read["dve"], 1)
                    elif kind == "v2":
                        b, c = s[1:]
                        up(dve, s_pv, G, 4 * NU, 4 * (BG + b - 1) if b >= 2 else 0)
                        V.tensor_copy(v2[b % 2][:, c, :, 0:HD], bank[0:SC, 0:C].rearrange("p (h d) -> p h d", h=H)).then_inc(s_read["dve"], 1)
                    elif kind == "max":
                        u, i = s[1:]
                        n = max_at[u, i]
                        up(dve, s_mxf, G, NMX, n + 1)
                        if i == 0:
                            up(dve, s_dg, G, 4 * NU, 4 * (u - 1) if u >= 2 else 0)
                        if u < BG:
                            V.tensor_reduce(negm[:, u % 2, i * GH:(i + 1) * GH], mxb[n % MAX_BANKS][0:T, 0:GH * T].rearrange("p (h s) -> p h s", h=GH),
                                            axis=AX_X, op=ALU.max, negate=True).then_inc(s_mx, 1)
                        else:
                            V.tensor_reduce(negm[:, u % 2, i:i + 1], mxb[n % MAX_BANKS][0:T, 0:S],
                                            axis=AX_X, op=ALU.max, negate=True).then_inc(s_mx, 1)
                    elif kind == "o1":
                        u = s[1]
                        heads = bank[0:T, :].rearrange("p (h x) -> p h x", h=H)
                        V.reciprocal(rden[:, :], heads[:, :, HD]).then_inc(s_rd, 1)
                        up(dve, s_rd, G, NU, u + 1)
                        up(dve, s_full, G, NMISC, misc_at["o2", u - 1] + 1 if u else 0)
                        V.tensor_tensor(att[:, :, :], heads[:, :, 0:HD], rden[:, :].unsqueeze(2).broadcast_to([T, H, HD]),
                                        ALU.mult).then_inc(s_read["dve"], 1)
                    elif kind == "o3":
                        u = s[1]
                        b = u % BG
                        if u < BG:
                            up(dve, s_res, G, 1, 1)
                            V.tensor_tensor(tb[:, b, :], bank[0:T, 0:C], tb[:, b, :], ALU.add).then_inc(s_read["dve"], 1)
                        else:
                            up(dve, s_resb, G, BG, b + 1)
                            up(dve, s_out[b % 2], G, 8 * BG, 16 * (b // 2))
                            V.tensor_tensor(ostage[:, b % 2, :], bank[0:T, 0:C], tb[:, b, :], ALU.add).then_inc(s_read["dve"], 1)

        @block.tensor
        def _(pe):
            count_ahead(pe, ahead_pe)
            M = nc.tensor.matmul
            pe.wait_ge(s_vec, 176)
            pe.wait_ge(s_w, 7 * 16)
            pe.wait_ge(s_init, 13)
            cols = [(raw_qkv, m * P, 0) for m in range(2 * KT)] + [(raw_kv, m * P, 1) for m in range(KT)]
            cols += [(raw_q2, m * P, 1) for m in range(KT)] + [(raw_f1, m * P, 2) for m in range(FT)]
            cols += [(raw_qkv, 2 * C + m * P, 0) for m in range(KT)] + [(raw_kv, C + m * P, 1) for m in range(KT)]
            for n, (raw, c0, i) in enumerate(cols):
                for k in range(KT):
                    mm = M(misc[0][:, n:n + 1], raw[:, k, c0:c0 + P], offs[:, i, k:k + 1], start=(k == 0), stop=(k == KT - 1))
            mm.then_inc(s_mcol, 1)
            pe.wait_ge(s_vbt, 1)
            for a, w in ((0, wps), (1, wpe)):
                for k in range(KT):
                    mm = M(misc[1][0:T, a * C:(a + 1) * C], vbt[:, a, k, :], w[:, k, :], start=(k == 0), stop=(k == KT - 1))
            mm.then_inc(s_mcol, 1)
            pe.wait_ge(s_flo, 4)

            def three_pass(dst, w_hi, w_lo, x_hi, x_lo):
                for k in range(KT):
                    M(dst, w_hi[:, k], x_hi[:, k], start=(k == 0), stop=False)
                    M(dst, w_hi[:, k], x_lo[:, k], start=False, stop=False)
                    mm = M(dst, w_lo[:, k], x_hi[:, k], start=False, stop=(k == KT - 1))
                return mm

            def plain(dst, xx, w):
                for k in range(KT):
                    mm = M(dst, xx[:, k], w[:, k], start=(k == 0), stop=(k == KT - 1))
                return mm

            with pe.Fori(0, GROUPS) as G:
                for s in steps:
                    kind = s[0]
                    bank = misc_bank(s) if kind in MISC_READER else None
                    if kind in MISC_READER and kind != "o3":
                        wait_misc_free(pe, G, s)
                    if kind == "xT":
                        k = s[1]
                        up(pe, s_norm, G, NLN, ln_at["ln1",] + 1)
                        for b in range(BG):
                            mm = nc.tensor.transpose(bank[:, b * T:(b + 1) * T], xn[:, b, k * P:(k + 1) * P], ident[0:T, 0:T])
                        mm.then_inc(s_full, 1)
                    elif kind == "qk1":
                        m = s[1]
                        up(pe, s_lo, G, NHL, hilo_at["split_x",] + 1)
                        c = slice(m * P, (m + 1) * P)
                        three_pass(bank[:, 0:NT], wqk_hi[:, :, c], wqk_lo[:, :, c], xT_hi, xT_lo).then_inc(s_full, 1)
                    elif kind == "v1":
                        b = s[1]
                        up(pe, s_read["act"], G, NREAD["act"], misc_read_count(("xT", KT - 1)))
                        plain(bank[0:T, 0:C], xT32[:, :, b * T:(b + 1) * T], wv1).then_inc(s_full, 1)
                    elif kind == "ff1":
                        m = s[1]
                        c = slice(m * P, (m + 1) * P)
                        three_pass(bank[:, 0:NT], wf1_hi[:, :, c], wf1_lo[:, :, c], xT_hi, xT_lo).then_inc(s_full, 1)
                    elif kind == "sT":
                        b, k = s[1:]
                        up(pe, s_norm, G, NLN, ln_at["ln_s", b] + 1)
                        for c in range(3):
                            mm = nc.tensor.transpose(bank[:, c * SC:(c + 1) * SC], xs[b % 2][:, c, k * P:(k + 1) * P], ident[0:SC, 0:SC])
                        mm.then_inc(s_full, 1)
                    elif kind == "k2":
                        b, m = s[1:]
                        up(pe, s_lo, G, NHL, hilo_at["split_s", b] + 1)
                        c = slice(m * P, (m + 1) * P)
                        three_pass(bank[:, 0:SP2], wk2_hi[:, :, c], wk2_lo[:, :, c], xsT_hi, xsT_lo).then_inc(s_full, 1)
                    elif kind == "v2":
                        b, c = s[1:]
                        plain(bank[0:SC, 0:C], xsT32[:, :, c * SC:(c + 1) * SC], wv2).then_inc(s_full, 1)
                    elif kind == "xq":
                        b = s[1]
                        up(pe, s_norm, G, NLN, ln_at["ln2", b] + 1)
                        for k in range(KT):
                            mm = nc.tensor.transpose(bank[:, k * T:(k + 1) * T], xn[:, b, k * P:(k + 1) * P], ident[0:T, 0:T])
                        mm.then_inc(s_full, 1)
                    elif kind == "q2":
                        m = s[1]
                        up(pe, s_lo, G, NHL, hilo_at["split_xq",] + 1)
                        c = slice(m * P, (m + 1) * P)
                        three_pass(bank[:, 0:NT], wq2_hi[:, :, c], wq2_lo[:, :, c], xT_hi, xT_lo).then_inc(s_full, 1)
                    elif kind == "max":
                        u, i = s[1:]
                        n = max_at[u, i]
                        mx = mxb[n % MAX_BANKS]
                        b = u % BG
                        up(pe, s_mx, G, NMX, n - MAX_BANKS + 1)
                        if i == 0 and u < BG:
                            up(pe, s_mask, G, 1, 1)
                            up(pe, s_qst, G, 2 * LAND, LAND)
                            up(pe, s_k1st, G, LAND, LAND)
                        elif i == 0:
                            up(pe, s_qst, G, 2 * LAND, 2 * LAND)
                            up(pe, s_k2st[b % 2], G, 2 * LAND, LAND * (b // 2 + 1))
                        if u < BG:
                            M(mx[0:T, 0:GH * T].rearrange("p (h s) -> p h s", h=GH), maskt[:, b, :],
                              identb[0:T, :].unsqueeze(1).broadcast_to([T, GH, T]), start=True, stop=False)
                            for j in range(GH):
                                h = i * GH + j
                                mm = M(mx[0:T, j * T:(j + 1) * T], qst[:, h, b * T:(b + 1) * T], k1st[:, h, b * T:(b + 1) * T],
                                       start=False, stop=(j == GH - 1))
                        else:
                            mm = M(mx[0:T, 0:S], qst[:, i, b * T:(b + 1) * T], k2st[b % 2][:, i, :], start=True, stop=True)
                        mm.then_inc(s_mxf, 1)
                    elif kind == "score":
                        u, g, c = s[1:]
                        n = score_at[u, g, c]
                        b = u % BG
                        rows = T if u < BG else SC
                        sc = scb[n % SCORE_BANKS]
                        up(pe, s_ex, G, NSC, n - SCORE_BANKS + 1)
                        up(pe, s_dg, G, 4 * NU, 4 * u + g + 1)
                        M(sc[0:rows, 0:GH * T], ones_t[:, 0:rows], diag[:, u % 2, g * GH * T:(g + 1) * GH * T], start=True, stop=False)
                        if u < BG:
                            M(sc[0:T, 0:GH * T].rearrange("p (h t) -> p h t", h=GH), identb[0:T, :],
                              maskt[:, b, :].unsqueeze(1).broadcast_to([T, GH, T]), start=False, stop=False)
                        for j in range(GH):
                            h = g * GH + j
                            ks = k1st[:, h, b * T:(b + 1) * T] if u < BG else k2st[b % 2][:, h, c * SC:(c + 1) * SC]
                            mm = M(sc[0:rows, j * T:(j + 1) * T], ks, qst[:, h, b * T:(b + 1) * T], start=False, stop=(j == GH - 1))
                        mm.then_inc(s_sc, 1)
                    elif kind == "pv":
                        u, g = s[1:]
                        b = u % BG
                        if g == 0:
                            up(pe, s_ot, G, NU, u)
                        if u < BG:
                            up(pe, s_read["dve"], G, NREAD["dve"], misc_read_count(("v1", b)))
                        else:
                            up(pe, s_read["dve"], G, NREAD["dve"], misc_read_count(("v2", b, 2)))
                        for c in range(chunks(u)):
                            n = score_at[u, g, c]
                            rows = T if u < BG else SC
                            up(pe, s_ex, G, NSC, n + 1)
                            for j in range(GH):
                                h = g * GH + j
                                vals = v1[:, b, h, :] if u < BG else v2[b % 2][:, c, h, :]
                                mm = M(pvb[32 * j:32 * j + VW, g * T:(g + 1) * T], vals,
                                       prob[0:rows, n % PROB_SLOTS, j * T:(j + 1) * T], start=(c == 0), stop=(c == chunks(u) - 1))
                        mm.then_inc(s_pv, 1)
                    elif kind == "o1":
                        u = s[1]
                        up(pe, s_ot, G, NU, u + 1)
                        for g in range(4):
                            mm = nc.tensor.transpose(bank[0:T, g * P:(g + 1) * P], ot[:, g * T:(g + 1) * T], ident[:, :])
                        mm.then_inc(s_full, 1)
                    elif kind == "o2":
                        u = s[1]
                        up(pe, s_read["dve"], G, NREAD["dve"], misc_read_count(("o1", u)))
                        for k in range(KT):
                            mm = nc.tensor.transpose(bank[:, k * T:(k + 1) * T], att[:, :, :].rearrange("p h d -> p (h d)")[:, k * P:(k + 1) * P], ident[0:T, 0:T])
                        mm.then_inc(s_full, 1)
                    elif kind == "ff2":
                        o3 = ("o3", s[1])
                        b = s[1] % BG
                        wait_misc_free(pe, G, o3)
                        up(pe, s_read["act"], G, NREAD["act"], misc_read_count(("ff1", FT - 1)))
                        for f in range(FT):
                            M(misc_bank(o3)[0:T, 0:C], hT[:, f, b * T:(b + 1) * T], wf2[:, f, :], start=(f == 0), stop=False)
                    elif kind == "o3":
                        u = s[1]
                        up(pe, s_read["act"], G, NREAD["act"], misc_read_count(("o2", u)))
                        if u < BG:
                            wait_misc_free(pe, G, s)
                        for k in range(KT):
                            mm = M(bank[0:T, 0:C], aT[:, k, :], (wps, wpe)[u // BG][:, k, :], start=(k == 0 and u < BG), stop=(k == KT - 1))
                        mm.then_inc(s_full, 1)


_WEIGHTS = ["sa_wqkv", "sa_wproj", "sa_bproj", "ed_wkv", "ed_wq", "ed_wproj", "ed_bproj", "ff_w1", "ff_b1", "ff_w2", "ff_b2",
            "ln1_g", "ln1_b", "ln2_g", "ln2_b", "ln3_g", "ln3_b"]


def kernel(**inputs):
    import numpy as _np
    import concourse.bacc as _bacc
    from concourse import mybir as _mybir
    from concourse.bass_utils import run_bass_kernel_spmd as _run

    maskT = _np.ascontiguousarray(_np.asarray(inputs["mask_BxS_bf0"]).T).view(_np.uint32)
    given = [("x", inputs["x"]), ("ctx", inputs["ctx_1024"]), ("maskT", maskT)]
    given += [(n, inputs["L0_xattn_" + n]) for n in _WEIGHTS]
    nc = _bacc.Bacc("TRN2", target_bir_lowering=False, num_devices=1)
    arrays, args = {}, []
    for name, a in given:
        a = _np.ascontiguousarray(a)
        arrays[f"in_{name}"] = a
        args.append(nc.dram_tensor(f"in_{name}", a.shape, _mybir.dt.from_np(a.dtype), kind="ExternalInput").ap())
    args.append(nc.dram_tensor("out_0", inputs["x"].shape, _mybir.dt.float32, kind="ExternalOutput").ap())
    layer_kernel(nc, *args)
    return _run(nc, [arrays], core_ids=[0]).results[0]["out_0"]
```

```python
from contextlib import ExitStack

import concourse.bass as bass
from concourse import mybir

F32 = mybir.dt.float32
F32R = mybir.dt.float32r
BF16 = mybir.dt.bfloat16
U8 = mybir.dt.uint8
U32 = mybir.dt.uint32
ALU = mybir.AluOpType
ACT = mybir.ActivationFunctionType
AX_X = mybir.AxisListType.X

P = 128
H = 16
BG = 4
EPS = 1e-5
MASKED = -1e30
SLOTS = 6
K_PART = (0, 1, 2, 0, 1, 0)
Q_PART = (0, 0, 0, 1, 1, 2)
MISC_BANKS, MAX_BANKS, SCORE_BANKS = 2, 3, 2
PROB_SLOTS = 6
LEAD = 2

MISC_READER = {"xT": "act", "qk1": "dve", "v1": "act", "ff1": "act", "sT": "act", "k2": "dve", "v2": "act", "ff2": "dve",
               "o1": "dve", "o2": "act", "o3": "dve", "xq": "act", "q2": "dve"}


def head_steps(kt):
    return [("load_tgt",), ("stats1",), ("norm1",)] + [("xT", k) for k in range(kt)] + [("split_x",)]


def group_steps(kt):
    nf = 4 * kt
    units = 2 * BG

    def chunks(u):
        return 1 if u < BG else 3

    quarters = [(u, g) for u in range(units) for g in range(4)]

    def maxima(u, g):
        heads = [g] if u < BG else range(4 * g, 4 * g + 4)
        return [[("max", u, i)] for i in heads] + [[("diag", u, g)]]

    def attention(first, last, fill, before_scores):
        qs = [q for q in quarters if first <= q[0] <= last]
        out = [x for q in qs[:LEAD] for part in maxima(*q) for x in part] + before_scores
        for n, (u, g) in enumerate(qs):
            ahead = maxima(*qs[n + LEAD]) if n + LEAD < len(qs) else []
            own = [[("score", u, g, c)] for c in range(chunks(u))]
            if n:
                own.insert(1, [("pv",) + qs[n - 1]] + ([("ot", qs[n - 1][0])] if qs[n - 1][1] == 3 else []))
            other = list(fill.get((u, g), []))
            while own or ahead or other:
                for parts in (own, ahead, other):
                    if parts:
                        out += parts.pop(0)
        return out + [("pv",) + qs[-1], ("ot", last)]

    def src_T(b):
        return [("sT", b, k) for k in range(kt)] + [("split_s", b)]

    def src_k(b):
        return [("k2", b, m) for m in range(kt)] + [("stack_k2", b)]

    def src_v(b):
        return [("v2", b, c) for c in range(3)]

    s = [("mask",), ("load_tb",), ("load_src", 0), ("load_src", 1)]
    s += [("qk1", 0), ("ff1", 0), ("qk1", 1), ("ff1", 1), ("stack_q1",), ("v1", 0), ("stats_s", 0)]
    s += [("qk1", 2), ("ff1", 2), ("v1", 1), ("qk1", 3), ("stack_k1",), ("ff1", 3), ("norm_s", 0), ("stats_s", 1)]
    s += [("v1", 2), ("v1", 3)] + [("resid",)] + src_T(0) + [("norm_s", 1), ("load_src", 2)]
    s += [("ff1", m) for m in range(4, nf - 2)] + [("k2", 0, 0), ("k2", 0, 1)]
    fill = {}
    for u in range(1, BG + 2):
        for g in range(4):
            fill[u, g] = []
    for u in range(BG):
        fill[u + 1, 1].insert(0, [("o1", u)])
        fill[u + 1, 2] += [[("o2", u)]]
        fill[u + 1, 3] += [[("o3", u), ("stats2", u)]]
        fill[u + 2, 0] += [[("norm2", u)]]
        fill[u + 2, 1] += [[("xq", u)]]
    s += attention(0, BG - 1, fill, [("stack_k2", 0), ("v2", 0, 0)])
    u = BG - 1
    s += [("norm2", u - 1), ("ff1", nf - 2), ("xq", u - 1), ("o1", u), ("ff1", nf - 1), ("o2", u), ("v2", 0, 1)]
    s += [("o3", u), ("stats2", u), ("v2", 0, 2), ("norm2", u), ("ff2", 0), ("xq", u), ("split_xq",)]
    s += src_T(1) + [("load_src", 3)] + [("q2", m) for m in range(kt)] + [("stack_q2",)]
    s += [("stats_s", 2), ("ff2", 1), ("norm_s", 2)] + src_k(1) + src_v(1) + [("load_tgt",)]
    fill = {}
    hd = head_steps(kt)
    for u in range(BG, units):
        b = u - BG
        f = [[], [], [], []]
        if b:
            f = [[], [[("o1", u - 1)]], [[("o2", u - 1)]], [[("o3", u - 1)]]]
        if b == 0:
            f[0] += [src_T(2)]
            f[1] += [[x] for x in src_k(2)]
            f[2] += [[x] for x in src_v(2)]
            f[3] += [[("stats_s", 3)]]
        elif b == 1:
            f[0] += [[("norm_s", 3)], src_T(3)]
            f[1] += [[x] for x in src_k(3)]
            f[2] += [[x] for x in src_v(3)]
        elif b == 2:
            f[0] += [[hd[1]]]
            f[1] += [[hd[2]]]
            f[2] += [[x] for x in hd[3:]]
        for g in range(4):
            fill[u, g] = f[g]
    s += attention(BG, units - 1, fill, [("ff2", 2)])
    u = units - 1
    s += [("ff2", 3), ("o1", u), ("o2", u), ("o3", u)]
    return s


class Order:

    def __init__(self, steps):
        self.steps = steps
        self.at = {s: i for i, s in enumerate(steps)}
        assert len(self.at) == len(steps)

    def of(self, *kinds):
        return [s for s in self.steps if s[0] in kinds]


def place_before(of_kind, step, size):
    n = of_kind.index(step)
    if n >= size:
        return of_kind[n - size]
    return of_kind[max(m for m in range(len(of_kind)) if m % size == n % size)]


def layer_kernel(nc, x, src, maskT, wqkv, sa_wproj, sa_bproj, ed_wkv, ed_wq, ed_wproj, ed_bproj,
                 ff_w1, ff_b1, ff_w2, ff_b2, g1, b1, g2, b2, g3, b3, out):
    B, T, C = x.shape
    S = src.shape[1]
    KT = C // P
    HD = C // H
    FT = ff_w1.shape[1] // P
    NT = BG * T
    SC = S // 3
    VW = HD + 1
    GH = 4
    SCALE = float(C) ** -0.5
    GROUPS = B // BG
    assert NT <= 512 and SC <= P and SC * 3 == S and GH * T <= 512 and FT == 4 * KT and H * HD == C
    SP2 = S + S % 2

    steps = group_steps(KT)
    head = head_steps(KT)
    od = Order(steps)
    miscs = od.of(*MISC_READER)
    scores = od.of("score")
    maxes = od.of("max")
    splits = od.of("qk1", "k2", "q2")
    q_stacks = od.of("stack_q1", "stack_q2")
    k_stacks = od.of("stack_k1", "stack_k2")
    stacks = od.of("stack_q1", "stack_q2", "stack_k1", "stack_k2")
    assert od.at["stack_q1",] < od.at["stack_q2",]
    LAND = 16 * SLOTS

    K2_PLACE = (0, 1, 2, 0)
    K2_BEFORE = (BG + 3, BG + 1, BG - 1, BG)

    NORMS = {"stats1": (0, BG, T), "norm1": (0, BG, T), "stats_s": (1, 3, SC), "norm_s": (1, 3, SC),
             "stats2": (2, 1, T), "norm2": (2, 1, T)}

    def chunks(u):
        return 1 if u < BG else 3

    with ExitStack() as ctx:
        def sb(name, shape, dt=F32):
            return ctx.enter_context(nc.sbuf_tensor(name, shape, dt))

        def ps(name, shape):
            return ctx.enter_context(nc.psum_tensor(name, shape, F32))

        def sem(name):
            return ctx.enter_context(nc.semaphore(name))

        wqk_hi = sb("wqk_hi", [P, KT, 2 * C], F32R)
        wqk_lo = sb("wqk_lo", [P, KT, 2 * C], F32R)
        wv1 = sb("wv1", [P, KT, C])
        wf1_hi = sb("wf1_hi", [P, KT, FT * P], F32R)
        wf1_lo = sb("wf1_lo", [P, KT, FT * P], F32R)
        wf2 = sb("wf2", [P, FT, C])
        wk2_hi = sb("wk2_hi", [P, KT, C], F32R)
        wk2_lo = sb("wk2_lo", [P, KT, C], F32R)
        wv2 = sb("wv2", [P, KT, C])
        wq2_hi = sb("wq2_hi", [P, KT, C], F32R)
        wq2_lo = sb("wq2_lo", [P, KT, C], F32R)
        wps = sb("wps", [P, KT, C])
        wpe = sb("wpe", [P, KT, C])
        gain = sb("gain", [P, 3, KT])
        offs = sb("offs", [P, 3, KT])
        bias1 = sb("bias1", [P, FT])
        NB = 2 * KT + KT + KT + FT
        bcol = sb("bcol", [P, NB])
        vb = sb("vb", [P, 2, KT])
        sab = sb("sab", [T, C])
        edb = sb("edb", [T, C])
        ident = sb("ident", [P, P])
        identb = sb("identb", [P, T], BF16)
        ones_t = sb("ones_t", [T, P], F32R)
        causal = sb("causal", [T, T])
        mhalf = sb("mhalf", [P, BG])
        epst = sb("epst", [P, BG])

        tb = sb("tb", [T, BG, C])
        xn = sb("xn", [T, BG, C])
        xT32 = sb("xT32", [P, KT, NT])
        xT_hi = sb("xT_hi", [P, KT, NT], F32R)
        xT_lo = sb("xT_lo", [P, KT, NT], F32R)
        hT = sb("hT", [P, FT, NT])
        qp = sb("qp", [P, KT, 3, NT], BF16)
        kp = sb("kp", [P, KT, 3, NT], BF16)
        rem = sb("rem", [P, 2, NT])
        qst = sb("qst", [P, H, NT], BF16)
        k1st = sb("k1st", [P, H, NT], BF16)
        k2flat = [sb(f"k2st{i}", [P, H * S], BF16) for i in range(2)]
        k2st = [f[:, :].rearrange("p (h s) -> p h s", h=H) for f in k2flat] + [k1st]
        v1 = sb("v1", [P, BG, H, VW])
        v2 = [sb(f"v2{i}", [SC, 3, H, VW]) for i in range(2)] + [v1]
        xs = [sb(f"xs{i}", [SC, 3, C]) for i in range(2)]
        xsT32 = sb("xsT32", [P, KT, SP2])
        xsT_hi = sb("xsT_hi", [P, KT, SP2], F32R)
        xsT_lo = sb("xsT_lo", [P, KT, SP2], F32R)
        stats = sb("stats", [P, 3, BG, 6])
        mv = sb("mv", [P, 3, BG, 2])
        veps = sb("veps", [P, 3, BG])
        rstd = sb("rstd", [P, 3, BG])
        assert BG == 4
        mask8 = sb("mask8", [T, B], U8)
        pad = sb("pad", [T, B])
        padneg = sb("padneg", [T, BG])
        maskt = sb("maskt", [T, BG, T], BF16)
        negm = sb("negm", [T, 2, H])
        diag = sb("diag", [T, 2, H * T], F32R)
        prob = sb("prob", [P, PROB_SLOTS, GH * T])
        ot = sb("ot", [P, GH * T])
        rden = sb("rden", [T, H])
        att = sb("att", [T, H, HD])
        aT = sb("aT", [P, KT, T])
        ostage = sb("ostage", [T, 2, C])

        hflat = hT[:, :, :].rearrange("p f n -> p (f n)")
        vbt = rem[:, :, :].rearrange("p a n -> p (a n)")[:, 0:2 * KT * T].rearrange("p (a k t) -> p a k t", a=2, k=KT)
        edb2 = ostage[:, 0, :]
        pflat = prob[:, :, :].rearrange("p s n -> p (s n)")
        raw_f1 = hflat[:, 0:KT * FT * P].rearrange("p (k n) -> p k n", k=KT)
        raw_qkv = hflat[:, KT * FT * P:KT * FT * P + KT * 3 * C].rearrange("p (k n) -> p k n", k=KT)
        raw_kv = pflat[:, 0:KT * 2 * C].rearrange("p (k n) -> p k n", k=KT)
        raw_q2 = pflat[:, KT * 2 * C:KT * 3 * C].rearrange("p (k n) -> p k n", k=KT)

        misc = [ps(f"misc{i}", [P, 512]) for i in range(MISC_BANKS)]
        mxb = [ps(f"mxb{i}", [P, 512]) for i in range(MAX_BANKS)]
        scb = [ps(f"scb{i}", [P, 512]) for i in range(SCORE_BANKS)]
        pvb = ps("pvb", [P, 512])

        scr_q = nc.dram_tensor("scr_q", (KT, P, 3, NT), BF16).ap()
        scr_k1 = nc.dram_tensor("scr_k1", (KT, P, 3, NT), BF16).ap()
        scr_k2 = [nc.dram_tensor(f"scr_k2{i}", (KT, P, 3, S), BF16).ap() for i in range(2)]

        s_w = sem("weights_landed")
        s_vec = sem("vectors_landed")
        s_const = sem("constants_made")
        s_init = sem("vector_constants_made")
        s_mcol = sem("prologue_matmuls_done")
        s_fold = sem("gain_folded")
        s_fhi = sem("folded_hi_made")
        s_flo = sem("folded_lo_made")
        s_bcol = sem("bias_columns_made")
        s_vbt = sem("value_offsets_spread")
        s_rows = sem("bias_rows_made")
        s_xt = sem("tgt_landed")
        s_tb = sem("residual_landed")
        s_xs = [sem(f"src_landed{i}") for i in range(2)]
        s_pad = sem("pad_terms_made")
        s_mask = sem("mask_tile_made")
        s_bn = sem("row_stats_made")
        s_mv = sem("mean_var_made")
        s_ve = sem("var_plus_eps_made")
        s_rs = sem("rstd_made")
        s_norm = sem("rows_normalised")
        s_res = sem("residual_started")
        s_resb = sem("residual_has_cross_bias")
        s_full = sem("misc_bank_filled")
        s_read = {"act": sem("misc_bank_read_by_act"), "dve": sem("misc_bank_read_by_dve")}
        s_hi = sem("hi_made")
        s_lo = sem("lo_made")
        s_p1 = sem("part1_made")
        s_p2 = sem("part2_made")
        s_p3 = sem("part3_made")
        s_step = sem("wait_holder")
        s_step_dve = sem("wait_holder_dve")
        s_scr = sem("parts_in_scratch")
        s_qst = sem("q_stack_landed")
        s_k1st = sem("k1_stack_landed")
        s_k2st = [sem(f"k2_stack_landed{b}") for b in range(BG)]
        s_mxf = sem("max_scores_made")
        s_mx = sem("max_made")
        s_dg = sem("diag_made")
        s_sc = sem("scores_made")
        s_ex = sem("probs_made")
        s_pv = sem("values_weighted")
        s_ot = sem("weighted_copied")
        s_rd = sem("reciprocals_made")
        s_out = [sem(f"output_stored{i}") for i in range(2)]

        signals = {}

        def signalled(s, by, each=1):
            signals[id(s)] = (by, each)

        signalled(s_full, miscs)
        for e in ("act", "dve"):
            signalled(s_read[e], [t for t in miscs if MISC_READER[t[0]] == e])
        for s in (s_mxf, s_mx):
            signalled(s, maxes)
        for s in (s_sc, s_ex):
            signalled(s, scores)
        for s in (s_p1, s_p2, s_p3):
            signalled(s, splits)
        for s in (s_bn, s_mv, s_ve, s_rs):
            signalled(s, od.of("stats1", "stats_s", "stats2"))
        signalled(s_norm, od.of("norm1", "norm_s", "norm2"))
        signalled(s_hi, od.of("split_xq"))
        signalled(s_lo, od.of("split_x", "split_s", "split_xq"))
        signalled(s_dg, od.of("diag"))
        signalled(s_pv, od.of("pv"))
        signalled(s_ot, od.of("ot"))
        signalled(s_rd, od.of("o1"))
        signalled(s_res, od.of("resid"))
        signalled(s_resb, od.of("norm2"))
        for s in (s_pad, s_mask):
            signalled(s, od.of("mask"))
        for b in range(BG):
            signalled(s_k2st[b], [("stack_k2", b)], LAND)
        signalled(s_xt, od.of("load_tgt"), 16)
        signalled(s_tb, od.of("load_tb"), 16)
        signalled(s_scr, stacks, 16 * KT)
        signalled(s_qst, q_stacks, LAND)
        signalled(s_k1st, od.of("stack_k1"), LAND)
        for i in range(2):
            signalled(s_xs[i], [t for t in od.of("load_src") if t[1] % 2 == i], 16)
            signalled(s_out[i], [t for t in od.of("o3") if t[1] >= BG and t[1] % 2 == i], 16)

        def after(eng, R, now, s, step):
            by, each = signals[id(s)]
            k = each * (by.index(step) + 1)
            if isinstance(R, int):
                if step not in head or od.at[step] > od.at[now]:
                    return
                k -= each * sum(t not in head for t in by[:by.index(step)])
                eng.wait_ge(s, each * sum(t not in head for t in by) + k)
            elif od.at[step] > od.at[now]:
                eng.wait_ge(s, R * (each * len(by)) - (each * len(by) - k))
            else:
                eng.wait_ge(s, R * (each * len(by)) + k)

        def count_group_before(eng, sems):
            for s in sems:
                by, each = signals[id(s)]
                n = each * sum(t not in head for t in by)
                if n:
                    eng.sem_inc(s, n)

        def head_done(eng):
            eng.wait_ge(s_lo, len(signals[id(s_lo)][0]))

        def split_of(step):
            kind, m = step[0], step[-1]
            if kind == "qk1" and m < KT:
                return qp[:, m], NT, m, place_before(q_stacks, ("stack_q1",), 1)
            if kind == "qk1":
                return kp[:, m - KT], NT, m, place_before(k_stacks, ("stack_k1",), 1)
            if kind == "q2":
                return qp[:, m], NT, 3 * KT + m, place_before(q_stacks, ("stack_q2",), 1)
            return kp[:, m], S, 2 * KT + m, place_before(k_stacks, ("stack_k2", step[1]), 1)

        def misc_bank(step):
            return misc[miscs.index(step) % MISC_BANKS]

        def wait_misc_free(pe, R, step):
            prev = place_before(miscs, step, MISC_BANKS)
            after(pe, R, step, s_read[MISC_READER[prev[0]]], prev)

        block = ctx.enter_context(nc.Block())

        @block.sync
        def _(sp):
            count_group_before(sp, [s_xt, s_tb, s_scr, s_qst, s_k1st, *s_xs, *s_k2st, *s_out])
            ctx.enter_context(nc.allow_non_contiguous_dma(reason="vectors by model dimension, mask bytes"))

            def w(dst, source):
                sp.dma_start(dst, source.rearrange("(k p) n -> p k n", p=P)).then_inc(s_w, 16)

            def v(dst, source):
                sp.dma_start(dst, source.rearrange("(k p) -> p k", p=P)).then_inc(s_vec, 16)

            def stack(R, s, parts, splits_of, scr, n, dst, part_of, landed, free=None):
                for m in range(KT):
                    after(sp, R, s, s_p3, splits_of[m])
                    sp.dma_start(scr[m, :, :, 0:n], parts[:, m, :, 0:n]).then_inc(s_scr, 16)
                after(sp, R, s, s_scr, s)
                if free is not None:
                    sp.sem_inc(s_step, 1)
                    after(sp, R, s, s_sc, free)
                for slot in range(SLOTS):
                    sp.dma_start(dst[HD * slot:HD * (slot + 1), :, 0:n],
                                 scr[:, :, part_of[slot], 0:n].rearrange("k (h d) t -> d (k h) t", d=HD)).then_inc(landed, 16)

            def transfers(R, s):
                kind = s[0]
                if kind == "load_tgt":
                    after(sp, R, s, s_full, ("xq", BG - 1))
                    b0 = 0 if isinstance(R, int) else (R % GROUPS) * BG
                    sp.dma_start(xn[:, :, :], x[bass.ds(b0, BG), :, :].rearrange("b t c -> t b c")).then_inc(s_xt, 16)
                elif kind == "load_tb":
                    after(sp, R, s, s_read["dve"], ("o3", 2 * BG - 1))
                    sp.dma_start(tb[:, :, :], x[bass.ds(R * BG - BG, BG), :, :].rearrange("b t c -> t b c")).then_inc(s_tb, 16)
                elif kind == "load_src":
                    b = s[1]
                    after(sp, R, s, s_full, ("sT", (b - 2) % BG, KT - 1))
                    sp.dma_start(xs[b % 2][:, :, :], src[bass.ds(R * BG - (BG - b), 1), :, :].rearrange("a (c s) n -> s (a c) n", c=3)).then_inc(s_xs[b % 2], 16)
                elif kind == "stack_q1":
                    stack(R, s, qp, [("qk1", m) for m in range(KT)], scr_q, NT, qst, Q_PART, s_qst)
                elif kind == "stack_k1":
                    stack(R, s, kp, [("qk1", KT + m) for m in range(KT)], scr_k1, NT, k1st, K_PART, s_k1st)
                elif kind == "stack_q2":
                    stack(R, s, qp, [("q2", m) for m in range(KT)], scr_q, NT, qst, Q_PART, s_qst)
                elif kind == "stack_k2":
                    b = s[1]
                    stack(R, s, kp, [("k2", b, m) for m in range(KT)], scr_k2[b % 2], S, k2st[K2_PLACE[b]], K_PART, s_k2st[b],
                          ("score", K2_BEFORE[b], 3, chunks(K2_BEFORE[b]) - 1))
                elif kind == "o3" and s[1] >= BG:
                    b = s[1] - BG
                    after(sp, R, s, s_read["dve"], s)
                    sp.dma_start(out[bass.ds(R * BG - (BG - b), 1), :, :].rearrange("a t c -> t (a c)"), ostage[:, b % 2, :]).then_inc(s_out[b % 2], 16)

            for s in head:
                transfers(0, s)
            w(raw_qkv, wqkv)
            for i, (g, b) in enumerate(((g1, b1), (g2, b2), (g3, b3))):
                v(gain[:, i, :], g)
                v(offs[:, i, :], b)
            v(bias1[:, :], ff_b1)
            sp.dma_start(mask8[:, :].bitcast(U32), maskT).then_inc(s_vec, 16)
            w(raw_kv, ed_wkv)
            w(raw_q2, ed_wq)
            w(raw_f1, ff_w1)
            w(wps[:, :, :], sa_wproj)
            w(wpe[:, :, :], ed_wproj)
            w(wf2[:, :, :], ff_w2)
            for dst, vec in ((sab[:, :], sa_bproj), (edb[:, :], ed_bproj), (edb2, ff_b2)):
                sp.dma_start(dst, vec.rearrange("(a n) -> a n", a=1).broadcast_to([T, C])).then_inc(s_vec, 16)
            head_done(sp)
            with sp.Fori(1, GROUPS + 1) as R:
                for s in steps:
                    transfers(R, s)
            for i in range(2):
                sp.wait_ge(s_out[i], 16 * (B + BG) // 2)
            sp.wait_ge(s_xt, 16 * (GROUPS + 1))

        @block.gpsimd
        def _(pool):
            count_group_before(pool, [s_ve, s_rs, s_dg, s_res, s_resb])
            nc.gpsimd.memset(ident[:, :], 0.0).then_inc(s_const, 1)
            nc.gpsimd.memset(causal[:, :], 0.0).then_inc(s_const, 1)
            nc.gpsimd.memset(mhalf[:, :], -0.5).then_inc(s_const, 1)
            nc.gpsimd.memset(epst[:, :], EPS).then_inc(s_const, 1)
            pool.wait_ge(s_const, 4)
            nc.gpsimd.affine_select(out=ident[:, :], in_=ident[:, :], compare_op=ALU.not_equal, fill=1.0,
                                    base=0, pattern=[[-1, P]], channel_multiplier=1).then_inc(s_const, 1)
            nc.gpsimd.affine_select(out=causal[:, :], in_=causal[:, :], compare_op=ALU.is_ge, fill=MASKED,
                                    base=0, pattern=[[1, T]], channel_multiplier=-1).then_inc(s_const, 1)
            for i in range(2):
                pool.wait_ge(s_const, 6 + i)
                nc.gpsimd.memset(k2flat[i][HD * SLOTS:P, :].bitcast(F32), 0.0).then_inc(s_const, 1)
            pool.wait_ge(s_const, 8)

            def pool_part(R, s):
                kind = s[0]
                if kind in NORMS and kind.startswith("stats"):
                    w, n, rows = NORMS[kind]
                    after(pool, R, s, s_mv, s)
                    nc.gpsimd.tensor_tensor(veps[0:rows, w, 0:n], mv[0:rows, w, 0:n, 1], epst[0:rows, 0:n], ALU.add).then_inc(s_ve, 1)
                    after(pool, R, s, s_ve, s)
                    nc.gpsimd.tensor_tensor(rstd[0:rows, w, 0:n], veps[0:rows, w, 0:n], mhalf[0:rows, 0:n], ALU.pow).then_inc(s_rs, 1)
                elif kind == "norm2":
                    b = s[1]
                    after(pool, R, s, s_norm, s)
                    nc.gpsimd.tensor_tensor(tb[:, b, :], tb[:, b, :], edb[:, :], ALU.add).then_inc(s_resb, 1)
                elif kind == "resid":
                    after(pool, R, s, s_tb, ("load_tb",))
                    nc.gpsimd.tensor_tensor(tb[:, :, :], tb[:, :, :], sab[:, :].unsqueeze(1).broadcast_to([T, BG, C]), ALU.add).then_inc(s_res, 1)
                elif kind == "diag":
                    u, g = s[1:]
                    after(pool, R, s, s_mx, ("max", u, g if u < BG else GH * g + GH - 1))
                    if g == 0:
                        o = (u - 2) % (2 * BG)
                        after(pool, R, s, s_sc, ("score", o, 3, chunks(o) - 1))
                    nc.gpsimd.tensor_tensor(diag[:, u % 2, g * GH * T:(g + 1) * GH * T].rearrange("p (h t) -> p h t", h=GH),
                                            ident[0:T, 0:T].unsqueeze(1).broadcast_to([T, GH, T]),
                                            negm[:, u % 2, g * GH:(g + 1) * GH].unsqueeze(2).broadcast_to([T, GH, T]),
                                            ALU.mult).then_inc(s_dg, 1)

            for s in head:
                pool_part(0, s)
            head_done(pool)
            pool.wait_ge(s_rows, 2)
            with pool.Fori(1, GROUPS + 1) as R:
                for s in steps:
                    pool_part(R, s)

        @block.scalar
        def _(act):
            count_group_before(act, [s_read["act"], s_ex, s_ot, s_p1])

            def act_part(R, s):
                kind = s[0]
                if MISC_READER.get(kind) == "act":
                    after(act, R, s, s_full, s)
                    bank = misc_bank(s)
                if kind == "xT":
                    k = s[1]
                    after(act, R, s, s_lo, ("split_xq",))
                    nc.scalar.activation(xT32[:, k, :], bank[:, 0:NT], ACT.Copy)
                    nc.scalar.activation(xT_hi[:, k, :], bank[:, 0:NT], ACT.Copy).then_inc(s_read["act"], 1)
                elif kind == "xq":
                    b = s[1]
                    after(act, R, s, s_lo, ("split_x",))
                    nc.scalar.activation(xT32[:, :, b * T:(b + 1) * T], bank[:, 0:KT * T].rearrange("p (k t) -> p k t", k=KT), ACT.Copy).then_inc(s_read["act"], 1)
                elif kind == "sT":
                    b, k = s[1:]
                    after(act, R, s, s_lo, ("split_s", (b - 1) % BG))
                    nc.scalar.activation(xsT32[:, k, 0:S], bank[:, 0:S], ACT.Copy)
                    nc.scalar.activation(xsT_hi[:, k, 0:S], bank[:, 0:S], ACT.Copy).then_inc(s_read["act"], 1)
                elif kind == "ff1":
                    m = s[1]
                    nc.scalar.activation(hT[:, m, :], bank[:, 0:NT], ACT.Relu, bias=bcol[:, 4 * KT + m:4 * KT + m + 1]).then_inc(s_read["act"], 1)
                elif kind == "v1":
                    b = s[1]
                    after(act, R, s, s_pv, ("pv", BG + 2, 3))
                    nc.scalar.activation(v1[0:T, b, :, 0:HD], bank[0:T, 0:C].rearrange("p (h d) -> p h d", h=H), ACT.Copy).then_inc(s_read["act"], 1)
                elif kind == "v2":
                    b, c = s[1:]
                    after(act, R, s, s_pv, ("pv", K2_BEFORE[b], 3))
                    nc.scalar.activation(v2[K2_PLACE[b]][0:SC, c, :, 0:HD], bank[0:SC, 0:C].rearrange("p (h d) -> p h d", h=H), ACT.Copy).then_inc(s_read["act"], 1)
                elif kind in ("qk1", "q2", "k2"):
                    parts, n, col, stack = split_of(s)
                    after(act, R, s, s_full, s)
                    after(act, R, s, s_scr, stack)
                    nc.scalar.activation(parts[:, 0, 0:n], misc_bank(s)[:, 0:n], ACT.Identity, bias=bcol[:, col:col + 1]).then_inc(s_p1, 1)
                elif kind == "o2":
                    u = s[1]
                    nc.scalar.activation(aT[:, :, :], bank[:, 0:KT * T].rearrange("p (k t) -> p k t", k=KT), ACT.Copy).then_inc(s_read["act"], 1)
                elif kind == "score":
                    n = scores.index(s)
                    rows = T if s[1] < BG else SC
                    after(act, R, s, s_sc, s)
                    old = place_before(scores, s, PROB_SLOTS)
                    after(act, R, s, s_pv, ("pv", old[1], old[2]))
                    nc.scalar.activation(prob[0:rows, n % PROB_SLOTS, :], scb[n % SCORE_BANKS][0:rows, 0:GH * T], ACT.Exp,
                                         scale=SCALE).then_inc(s_ex, 1)
                elif kind == "ot":
                    u = s[1]
                    after(act, R, s, s_pv, ("pv", u, 3))
                    after(act, R, s, s_full, ("o1", (u - 1) % (2 * BG)))
                    nc.scalar.activation(ot[:, :], pvb[:, 0:GH * T], ACT.Copy).then_inc(s_ot, 1)

            for s in head:
                act_part(0, s)
            head_done(act)
            act.wait_ge(s_rows, 2)
            with act.Fori(1, GROUPS + 1) as R:
                for s in steps:
                    act_part(R, s)

        @block.vector
        def _(dve):
            count_group_before(dve, [s_read["dve"], s_p2, s_p3, s_bn, s_mv, s_norm, s_hi, s_lo, s_mx, s_rd, s_pad, s_mask])
            V = nc.vector
            def row_stats(R, s, row_set):
                w, n, rows = NORMS[s[0]]
                for j in range(n):
                    i = V.bn_stats(stats[0:rows, w, j, :], row_set(j))
                i.then_inc(s_bn, 1)
                after(dve, R, s, s_bn, s)
                dve.sem_inc(s_step_dve, 1)
                for j in range(n):
                    i = V.bn_aggr(mv[0:rows, w, j, :], stats[0:rows, w, j, :])
                i.then_inc(s_mv, 1)

            def normalise(R, s, stats_step, from_set, to_set):
                w, n, rows = NORMS[s[0]]
                after(dve, R, s, s_rs, stats_step)
                for j in range(n):
                    i = V.tensor_scalar(to_set(j), from_set(j), mv[0:rows, w, j, 0:1], rstd[0:rows, w, j:j + 1], ALU.subtract, ALU.mult)
                i.then_inc(s_norm, 1)

            def lo_part(x32, hi, lo):
                V.tensor_tensor(lo, x32, hi.bitcast(F32), ALU.subtract).then_inc(s_lo, 1)

            def split3(R, s, bank, n, bias, parts, r):
                after(dve, R, s, s_p1, s)
                V.scalar_tensor_tensor(r[:, 0:n], bank[:, 0:n], bias, parts[:, 0, 0:n], ALU.add, ALU.subtract).then_inc(s_read["dve"], 1)
                after(dve, R, s, s_read["dve"], s)
                V.tensor_copy(parts[:, 1, 0:n], r[:, 0:n]).then_inc(s_p2, 1)
                after(dve, R, s, s_p2, s)
                V.tensor_tensor(parts[:, 2, 0:n], r[:, 0:n], parts[:, 1, 0:n], ALU.subtract).then_inc(s_p3, 1)

            def dve_part(R, s):
                kind = s[0]
                if MISC_READER.get(kind) == "dve":
                    if kind not in ("qk1", "k2", "q2"):
                        after(dve, R, s, s_full, s)
                    bank = misc_bank(s)
                if kind == "mask":
                    V.tensor_copy(padneg[:, :], pad[:, bass.ds(R * BG - BG, BG)]).then_inc(s_pad, 1)
                    after(dve, R, s, s_pad, s)
                    after(dve, R, s, s_sc, ("score", BG - 1, 3, 0))
                    for b in range(BG):
                        i = V.tensor_scalar(maskt[:, b, :], causal[:, :], padneg[:, b:b + 1], None, ALU.add)
                    i.then_inc(s_mask, 1)
                elif kind == "stats1":
                    after(dve, R, s, s_xt, ("load_tgt",))
                    row_stats(R, s, lambda j: xn[:, j, :])
                elif kind == "norm1":
                    normalise(R, s, ("stats1",), lambda j: xn[:, j, :], lambda j: xn[:, j, :])
                elif kind == "stats_s":
                    b = s[1]
                    after(dve, R, s, s_xs[b % 2], ("load_src", b))
                    row_stats(R, s, lambda j: xs[b % 2][:, j, :])
                elif kind == "norm_s":
                    b = s[1]
                    normalise(R, s, ("stats_s", b), lambda j: xs[b % 2][:, j, :], lambda j: xs[b % 2][:, j, :])
                elif kind == "stats2":
                    b = s[1]
                    after(dve, R, s, s_read["dve"], ("o3", b))
                    row_stats(R, s, lambda j: tb[:, b, :])
                elif kind == "norm2":
                    b = s[1]
                    after(dve, R, s, s_full, ("xT", KT - 1))
                    normalise(R, s, ("stats2", b), lambda j: tb[:, b, :], lambda j: xn[:, b, :])
                elif kind == "split_x":
                    after(dve, R, s, s_read["act"], ("xT", KT - 1))
                    after(dve, R, s, s_full, ("q2", KT - 1))
                    lo_part(xT32[:, :, :], xT_hi[:, :, :], xT_lo[:, :, :])
                elif kind == "split_s":
                    b = s[1]
                    after(dve, R, s, s_read["act"], ("sT", b, KT - 1))
                    after(dve, R, s, s_full, ("k2", (b - 1) % BG, KT - 1))
                    lo_part(xsT32[:, :, :], xsT_hi[:, :, :], xsT_lo[:, :, :])
                elif kind == "split_xq":
                    after(dve, R, s, s_read["act"], ("xq", BG - 1))
                    after(dve, R, s, s_full, ("ff1", FT - 1))
                    V.tensor_copy(xT_hi[:, :, :], xT32[:, :, :]).then_inc(s_hi, 1)
                    after(dve, R, s, s_hi, s)
                    lo_part(xT32[:, :, :], xT_hi[:, :, :], xT_lo[:, :, :])
                elif kind in ("qk1", "q2", "k2"):
                    parts, n, col, _ = split_of(s)
                    split3(R, s, bank, n, bcol[:, col:col + 1], parts, rem[:, splits.index(s) % 2])
                elif kind == "max":
                    u, i = s[1:]
                    mx = mxb[maxes.index(s) % MAX_BANKS]
                    after(dve, R, s, s_mxf, s)
                    if i == 0:
                        after(dve, R, s, s_dg, ("diag", (u - 2) % (2 * BG), 3))
                    if u < BG:
                        V.tensor_reduce(negm[:, u % 2, i * GH:(i + 1) * GH], mx[0:T, 0:GH * T].rearrange("p (h s) -> p h s", h=GH),
                                        axis=AX_X, op=ALU.max, negate=True).then_inc(s_mx, 1)
                    else:
                        V.tensor_reduce(negm[:, u % 2, i:i + 1], mx[0:T, 0:S],
                                        axis=AX_X, op=ALU.max, negate=True).then_inc(s_mx, 1)
                elif kind == "o1":
                    u = s[1]
                    heads = bank[0:T, :].rearrange("p (h x) -> p h x", h=H)
                    V.reciprocal(rden[:, :], heads[:, :, HD]).then_inc(s_rd, 1)
                    after(dve, R, s, s_rd, s)
                    V.tensor_tensor(att[:, :, :], heads[:, :, 0:HD], rden[:, :].unsqueeze(2).broadcast_to([T, H, HD]),
                                    ALU.mult).then_inc(s_read["dve"], 1)
                elif kind == "ff2":
                    b = s[1]
                    after(dve, R, s, s_resb, ("norm2", b))
                    V.tensor_tensor(tb[:, b, :], bank[0:T, 0:C], tb[:, b, :], ALU.add).then_inc(s_read["dve"], 1)
                elif kind == "o3":
                    u = s[1]
                    b = u % BG
                    if u < BG:
                        after(dve, R, s, s_res, ("resid",))
                        V.tensor_tensor(tb[:, b, :], bank[0:T, 0:C], tb[:, b, :], ALU.add).then_inc(s_read["dve"], 1)
                    else:
                        after(dve, R, s, s_read["dve"], ("ff2", b))
                        after(dve, R, s, s_out[b % 2], ("o3", BG + (b - 2) % BG))
                        V.tensor_tensor(ostage[:, b % 2, :], bank[0:T, 0:C], tb[:, b, :], ALU.add).then_inc(s_read["dve"], 1)
            for s in head:
                dve_part(0, s)
            V.memset(ones_t[:, :].bitcast(F32), 1.0).then_inc(s_init, 1)
            V.memset(pvb[:, :], 0.0).then_inc(s_init, 1)
            V.memset(v1[:, :, :, HD:VW], 1.0).then_inc(s_init, 1)
            for i in range(2):
                V.memset(v2[i][:, :, :, HD:VW], 1.0).then_inc(s_init, 1)
            V.memset(qst[HD * SLOTS:P, :, :].bitcast(F32), 0.0).then_inc(s_init, 1)
            V.memset(k1st[HD * SLOTS:P, :, :].bitcast(F32), 0.0).then_inc(s_init, 1)
            V.memset(xsT32[:, :, :], 0.0).then_inc(s_init, 1)
            V.memset(xsT_hi[:, :, :].bitcast(F32), 0.0).then_inc(s_init, 1)
            dve.wait_ge(s_const, 8)
            V.tensor_copy(identb[0:T, :], ident[0:T, 0:T]).then_inc(s_init, 1)
            dve.wait_ge(s_vec, 176)
            dve.wait_ge(s_w, 7 * 16)
            V.tensor_tensor(edb[:, :], edb[:, :], edb2, ALU.add).then_inc(s_init, 1)
            V.tensor_scalar(pad[:, :], mask8[:, :], MASKED, None, ALU.mult).then_inc(s_init, 1)
            for k in range(KT):
                V.tensor_scalar(wv1[:, k, :], raw_qkv[:, k, 2 * C:3 * C], gain[:, 0, k:k + 1], None, ALU.mult).then_inc(s_init, 1)
                V.tensor_scalar(wv2[:, k, :], raw_kv[:, k, C:2 * C], gain[:, 1, k:k + 1], None, ALU.mult).then_inc(s_init, 1)
            dve.wait_ge(s_mcol, 1)
            folds = ((raw_qkv[:, :, 0:2 * C], 0, wqk_hi, wqk_lo), (raw_kv[:, :, 0:C], 1, wk2_hi, wk2_lo),
                     (raw_q2, 1, wq2_hi, wq2_lo), (raw_f1, 2, wf1_hi, wf1_lo))
            for n, (raw, i, hi, lo) in enumerate(folds):
                for k in range(KT):
                    V.tensor_scalar(raw[:, k, :], raw[:, k, :], gain[:, i, k:k + 1], None, ALU.mult).then_inc(s_fold, 1)
                dve.wait_ge(s_fold, KT * (n + 1))
                V.tensor_copy(hi[:, :, :], raw).then_inc(s_fhi, 1)
                dve.wait_ge(s_fhi, n + 1)
                V.tensor_tensor(lo[:, :, :], raw, hi[:, :, :].bitcast(F32), ALU.subtract).then_inc(s_flo, 1)
            V.tensor_copy(bcol[:, 0:4 * KT], misc[0][:, 0:4 * KT]).then_inc(s_bcol, 1)
            V.tensor_tensor(bcol[:, 4 * KT:NB], misc[0][:, 4 * KT:NB], bias1[:, :], ALU.add).then_inc(s_bcol, 1)
            V.tensor_copy(vb[:, :, :], misc[0][:, NB:NB + 2 * KT].rearrange("p (a k) -> p a k", a=2)).then_inc(s_bcol, 1)
            dve.wait_ge(s_bcol, 3)
            V.tensor_copy(vbt[:, :, :, :], vb[:, :, :].unsqueeze(3).broadcast_to([P, 2, KT, T])).then_inc(s_vbt, 1)
            dve.wait_ge(s_mcol, 2)
            dve.wait_ge(s_init, 12)
            V.tensor_tensor(sab[:, :], misc[1][0:T, 0:C], sab[:, :], ALU.add).then_inc(s_rows, 1)
            V.tensor_tensor(edb[:, :], misc[1][0:T, C:2 * C], edb[:, :], ALU.add).then_inc(s_rows, 1)

            with dve.Fori(1, GROUPS + 1) as R:
                for s in steps:
                    dve_part(R, s)

        @block.tensor
        def _(pe):
            count_group_before(pe, [s_full, s_mxf, s_sc, s_pv])
            M = nc.tensor.matmul
            def three_pass(dst, w_hi, w_lo, x_hi, x_lo):
                for k in range(KT):
                    M(dst, w_hi[:, k], x_hi[:, k], start=(k == 0), stop=False)
                    M(dst, w_hi[:, k], x_lo[:, k], start=False, stop=False)
                    mm = M(dst, w_lo[:, k], x_hi[:, k], start=False, stop=(k == KT - 1))
                return mm

            def plain(dst, xx, w):
                for k in range(KT):
                    mm = M(dst, xx[:, k], w[:, k], start=(k == 0), stop=(k == KT - 1))
                return mm

            def pe_part(R, s):
                kind = s[0]
                if kind in MISC_READER:
                    wait_misc_free(pe, R, s)
                    bank = misc_bank(s)
                if kind == "xT":
                    k = s[1]
                    after(pe, R, s, s_norm, ("norm1",))
                    for b in range(BG):
                        mm = nc.tensor.transpose(bank[:, b * T:(b + 1) * T], xn[:, b, k * P:(k + 1) * P], ident[0:T, 0:T])
                    mm.then_inc(s_full, 1)
                elif kind == "qk1":
                    m = s[1]
                    after(pe, R, s, s_lo, ("split_x",))
                    c = slice(m * P, (m + 1) * P)
                    three_pass(bank[:, 0:NT], wqk_hi[:, :, c], wqk_lo[:, :, c], xT_hi, xT_lo).then_inc(s_full, 1)
                elif kind == "v1":
                    b = s[1]
                    after(pe, R, s, s_read["act"], ("xT", KT - 1))
                    plain(bank[0:T, 0:C], xT32[:, :, b * T:(b + 1) * T], wv1).then_inc(s_full, 1)
                elif kind == "ff1":
                    m = s[1]
                    c = slice(m * P, (m + 1) * P)
                    three_pass(bank[:, 0:NT], wf1_hi[:, :, c], wf1_lo[:, :, c], xT_hi, xT_lo).then_inc(s_full, 1)
                elif kind == "sT":
                    b, k = s[1:]
                    after(pe, R, s, s_norm, ("norm_s", b))
                    for c in range(3):
                        mm = nc.tensor.transpose(bank[:, c * SC:(c + 1) * SC], xs[b % 2][:, c, k * P:(k + 1) * P], ident[0:SC, 0:SC])
                    mm.then_inc(s_full, 1)
                elif kind == "k2":
                    b, m = s[1:]
                    after(pe, R, s, s_lo, ("split_s", b))
                    c = slice(m * P, (m + 1) * P)
                    three_pass(bank[:, 0:SP2], wk2_hi[:, :, c], wk2_lo[:, :, c], xsT_hi, xsT_lo).then_inc(s_full, 1)
                elif kind == "v2":
                    b, c = s[1:]
                    after(pe, R, s, s_read["act"], ("sT", b, KT - 1))
                    plain(bank[0:SC, 0:C], xsT32[:, :, c * SC:(c + 1) * SC], wv2).then_inc(s_full, 1)
                elif kind == "xq":
                    b = s[1]
                    after(pe, R, s, s_norm, ("norm2", b))
                    for k in range(KT):
                        mm = nc.tensor.transpose(bank[:, k * T:(k + 1) * T], xn[:, b, k * P:(k + 1) * P], ident[0:T, 0:T])
                    mm.then_inc(s_full, 1)
                elif kind == "q2":
                    m = s[1]
                    after(pe, R, s, s_lo, ("split_xq",))
                    c = slice(m * P, (m + 1) * P)
                    three_pass(bank[:, 0:NT], wq2_hi[:, :, c], wq2_lo[:, :, c], xT_hi, xT_lo).then_inc(s_full, 1)
                elif kind == "max":
                    u, i = s[1:]
                    mx = mxb[maxes.index(s) % MAX_BANKS]
                    b = u % BG
                    after(pe, R, s, s_mx, place_before(maxes, s, MAX_BANKS))
                    if i == 0 and u < BG:
                        after(pe, R, s, s_mask, ("mask",))
                        after(pe, R, s, s_qst, ("stack_q1",))
                        after(pe, R, s, s_k1st, ("stack_k1",))
                    elif i == 0:
                        after(pe, R, s, s_qst, ("stack_q2",))
                        after(pe, R, s, s_k2st[b], ("stack_k2", b))
                    if u < BG:
                        M(mx[0:T, 0:GH * T].rearrange("p (h s) -> p h s", h=GH), maskt[:, b, :],
                          identb[0:T, :].unsqueeze(1).broadcast_to([T, GH, T]), start=True, stop=False)
                        for j in range(GH):
                            h = i * GH + j
                            mm = M(mx[0:T, j * T:(j + 1) * T], qst[:, h, b * T:(b + 1) * T], k1st[:, h, b * T:(b + 1) * T],
                                   start=False, stop=(j == GH - 1))
                    else:
                        mm = M(mx[0:T, 0:S], qst[:, i, b * T:(b + 1) * T], k2st[K2_PLACE[b]][:, i, 0:S], start=True, stop=True)
                    mm.then_inc(s_mxf, 1)
                elif kind == "score":
                    u, g, c = s[1:]
                    b = u % BG
                    rows = T if u < BG else SC
                    sc = scb[scores.index(s) % SCORE_BANKS]
                    after(pe, R, s, s_ex, place_before(scores, s, SCORE_BANKS))
                    after(pe, R, s, s_dg, ("diag", u, g))
                    M(sc[0:rows, 0:GH * T], ones_t[:, 0:rows], diag[:, u % 2, g * GH * T:(g + 1) * GH * T], start=True, stop=False)
                    if u < BG:
                        M(sc[0:T, 0:GH * T].rearrange("p (h t) -> p h t", h=GH), identb[0:T, :],
                          maskt[:, b, :].unsqueeze(1).broadcast_to([T, GH, T]), start=False, stop=False)
                    for j in range(GH):
                        h = g * GH + j
                        ks = k1st[:, h, b * T:(b + 1) * T] if u < BG else k2st[K2_PLACE[b]][:, h, c * SC:(c + 1) * SC]
                        mm = M(sc[0:rows, j * T:(j + 1) * T], ks, qst[:, h, b * T:(b + 1) * T], start=False, stop=(j == GH - 1))
                    mm.then_inc(s_sc, 1)
                elif kind == "pv":
                    u, g = s[1:]
                    b = u % BG
                    if g == 0:
                        after(pe, R, s, s_ot, ("ot", (u - 1) % (2 * BG)))
                    after(pe, R, s, s_read["act"], ("v1", b) if u < BG else ("v2", b, 2))
                    for c in range(chunks(u)):
                        after(pe, R, s, s_ex, ("score", u, g, c))
                        slot = scores.index(("score", u, g, c)) % PROB_SLOTS
                        rows = T if u < BG else SC
                        for j in range(GH):
                            h = g * GH + j
                            vals = v1[0:T, b, h, :] if u < BG else v2[K2_PLACE[b]][0:SC, c, h, :]
                            mm = M(pvb[32 * j:32 * j + VW, g * T:(g + 1) * T], vals,
                                   prob[0:rows, slot, j * T:(j + 1) * T], start=(c == 0), stop=(c == chunks(u) - 1))
                    mm.then_inc(s_pv, 1)
                elif kind == "o1":
                    u = s[1]
                    after(pe, R, s, s_ot, ("ot", u))
                    for g in range(4):
                        mm = nc.tensor.transpose(bank[0:T, g * P:(g + 1) * P], ot[:, g * T:(g + 1) * T], ident[:, :])
                    mm.then_inc(s_full, 1)
                elif kind == "o2":
                    u = s[1]
                    after(pe, R, s, s_read["dve"], ("o1", u))
                    for k in range(KT):
                        mm = nc.tensor.transpose(bank[:, k * T:(k + 1) * T], att[:, :, :].rearrange("p h d -> p (h d)")[:, k * P:(k + 1) * P], ident[0:T, 0:T])
                    mm.then_inc(s_full, 1)
                elif kind == "ff2":
                    b = s[1]
                    after(pe, R, s, s_read["act"], ("ff1", FT - 1))
                    for f in range(FT):
                        mm = M(bank[0:T, 0:C], hT[:, f, b * T:(b + 1) * T], wf2[:, f, :], start=(f == 0), stop=(f == FT - 1))
                    mm.then_inc(s_full, 1)
                elif kind == "o3":
                    u = s[1]
                    after(pe, R, s, s_read["act"], ("o2", u))
                    for k in range(KT):
                        mm = M(bank[0:T, 0:C], aT[:, k, :], (wps, wpe)[u // BG][:, k, :], start=(k == 0), stop=(k == KT - 1))
                    mm.then_inc(s_full, 1)
            pe.wait_ge(s_const, 8)
            for s in head:
                pe_part(0, s)
            head_done(pe)
            pe.wait_ge(s_vec, 176)
            pe.wait_ge(s_w, 7 * 16)
            pe.wait_ge(s_init, 12)
            cols = [(raw_qkv, m * P, 0) for m in range(2 * KT)] + [(raw_kv, m * P, 1) for m in range(KT)]
            cols += [(raw_q2, m * P, 1) for m in range(KT)] + [(raw_f1, m * P, 2) for m in range(FT)]
            cols += [(raw_qkv, 2 * C + m * P, 0) for m in range(KT)] + [(raw_kv, C + m * P, 1) for m in range(KT)]
            for n, (raw, c0, i) in enumerate(cols):
                for k in range(KT):
                    mm = M(misc[0][:, n:n + 1], raw[:, k, c0:c0 + P], offs[:, i, k:k + 1], start=(k == 0), stop=(k == KT - 1))
            mm.then_inc(s_mcol, 1)
            pe.wait_ge(s_vbt, 1)
            for a, w in ((0, wps), (1, wpe)):
                for k in range(KT):
                    mm = M(misc[1][0:T, a * C:(a + 1) * C], vbt[:, a, k, :], w[:, k, :], start=(k == 0), stop=(k == KT - 1))
            mm.then_inc(s_mcol, 1)
            pe.wait_ge(s_rows, 2)

            with pe.Fori(1, GROUPS + 1) as R:
                for s in steps:
                    pe_part(R, s)


_WEIGHTS = ["sa_wqkv", "sa_wproj", "sa_bproj", "ed_wkv", "ed_wq", "ed_wproj", "ed_bproj", "ff_w1", "ff_b1", "ff_w2", "ff_b2",
            "ln1_g", "ln1_b", "ln2_g", "ln2_b", "ln3_g", "ln3_b"]


def kernel(**inputs):
    import numpy as _np
    import concourse.bacc as _bacc
    from concourse import mybir as _mybir
    from concourse.bass_utils import run_bass_kernel_spmd as _run

    maskT = _np.ascontiguousarray(_np.asarray(inputs["mask_BxS_bf0"]).T).view(_np.uint32)
    given = [("x", inputs["x"]), ("ctx", inputs["ctx_1024"]), ("maskT", maskT)]
    given += [(n, inputs["L0_xattn_" + n]) for n in _WEIGHTS]
    nc = _bacc.Bacc("TRN2", target_bir_lowering=False, num_devices=1)
    arrays, args = {}, []
    for name, a in given:
        a = _np.ascontiguousarray(a)
        arrays[f"in_{name}"] = a
        args.append(nc.dram_tensor(f"in_{name}", a.shape, _mybir.dt.from_np(a.dtype), kind="ExternalInput").ap())
    args.append(nc.dram_tensor("out_0", inputs["x"].shape, _mybir.dt.float32, kind="ExternalOutput").ap())
    layer_kernel(nc, *args)
    return _run(nc, [arrays], core_ids=[0]).results[0]["out_0"]
```

```python
from contextlib import ExitStack
from itertools import zip_longest

import concourse.bass as bass
from concourse import mybir

F32 = mybir.dt.float32
F32R = mybir.dt.float32r
BF16 = mybir.dt.bfloat16
U8 = mybir.dt.uint8
U32 = mybir.dt.uint32
ALU = mybir.AluOpType
ACT = mybir.ActivationFunctionType
AX_X = mybir.AxisListType.X

P = 128
H = 16
BG = 4
EPS = 1e-5
MASKED = -1e30
SLOTS = 6
K_PART = (0, 1, 2, 0, 1, 0)
Q_PART = (0, 0, 0, 1, 1, 2)
MISC_BANKS, MAX_BANKS, SCORE_BANKS = 2, 3, 2
PROB_SLOTS = 5
FF2_PIECES = 2
LEAD = 4

MISC_READER = {"xT": "act", "qk1": "dve", "v1": "act", "ff1": "act", "sT": "act", "k2": "dve", "v2": "act", "ff2": "dve",
               "o1": "dve", "o2": "act", "o3": "dve", "xq": "dve", "mT": "act", "q2": "dve"}

UNITS = (2, 3, 4, 5, 0, 1, 6, 7)


def chunks(u):
    return 1 if u < BG else 3


def other_work(kt):
    fill = {
        (2, 0): [("load_tgt",), ("load_tb", 1), [("sT", 1, 0), ("sT", 1, 1), ("split_s", 1)]],
        (2, 1): [("ff1", 4), ("k2", 1, 0), ("resid", 1), ("k2", 1, 1), ("stack_k2", 1)],
        (2, 2): [("v2", 1, 0), ("v2", 1, 1), ("ff1", 6), ("ff1", 5), ("stats1",)],
        (2, 3): [],
        (3, 0): [("norm1",), ("ff1", 7), ("load_src", 3)],
        (3, 1): [("o1", 2), [("xT", 0), ("xT", 1), ("split_x",)], ("v2", 1, 2)],
        (3, 2): [("o2", 2), ("qk1", 0), ("ff2", 0), ("qk1", 1)],
        (3, 3): [("qk1", 2), ("qk1", 3), ("ff2", 1)],
        (4, 0): [[("o3", 2), ("stats2", 2)], ("stack_q1",), ("stack_k1",), ("mask",)],
        (4, 1): [("o1", 3), ("norm2", 2)],
        (4, 2): [("o2", 3), ("stats_s", 2), [("o3", 3), ("stats2", 3)]],
        (4, 3): [("norm_s", 2), ("norm2", 3), ("xq", 2)],
        (5, 0): [[("sT", 2, 0), ("sT", 2, 1), ("split_s", 2)], ("xq", 3), ("stats_s", 3)],
        (5, 1): [("q2", 1, 0), ("o1", 4), ("k2", 2, 0), ("q2", 1, 1), ("stack_q2", 1), ("k2", 2, 1), ("stack_k2", 2)],
        (5, 2): [("v2", 2, 0), ("o2", 4), ("v2", 2, 1), ("norm_s", 3), ("v1", 0)],
        (5, 3): [("o3", 4), ("v2", 2, 2), ("load_src", 0), ("v1", 1)],
        (0, 0): [[("sT", 3, 0), ("sT", 3, 1), ("split_s", 3)]],
        (0, 1): [("o1", 5), ("k2", 3, 0), ("k2", 3, 1)],
        (0, 2): [("stack_k2", 3), ("v2", 3, 0), ("o2", 5), ("v2", 3, 1)],
        (0, 3): [("load_src", 1), ("ff2", 2)],
        (1, 0): [],
        (1, 1): [("o1", 0), ("o3", 5), ("load_tb", 0), ("ff2", 3), ("o2", 0), ("resid", 0)],
        (1, 2): [],
        (1, 3): [("v2", 3, 2), [("o3", 0), ("stats2", 0)]],
        (6, 0): [("ff1", 1), ("norm2", 0)],
        (6, 1): [("o1", 1), ("xq", 0)],
        (6, 2): [("stats_s", 0), ("o2", 1), [("o3", 1), ("stats2", 1)], ("ff1", 2)],
        (6, 3): [("norm2", 1), ("ff1", 0), ("norm_s", 0), ("xq", 1)],
        (7, 0): [[("sT", 0, 0), ("sT", 0, 1), ("split_s", 0)]],
        (7, 1): [("q2", 0, 0), ("o1", 6), ("q2", 0, 1), ("k2", 0, 0), ("stack_q2", 0), ("ff1", 3), ("k2", 0, 1)],
        (7, 2): [("o2", 6), ("stats_s", 1), ("v2", 0, 0), ("v2", 0, 1)],
        (7, 3): [("o3", 6), ("stack_k2", 0), ("norm_s", 1), ("v2", 0, 2), ("load_src", 2)],
    }
    return {q: [[t] if isinstance(t, tuple) else t for t in parts] for q, parts in fill.items()}


def period_steps(kt):
    nf = 4 * kt
    quarters = [(u, g) for u in UNITS for g in range(4)]

    def maxima(u, g):
        heads = [g] if u < BG else range(4 * g, 4 * g + 4)
        return [[("max", u, i)] for i in heads] + ([[("max_parts", u, g // 2)]] if g % 2 else [])

    fill = other_work(kt)
    s, ready = [], []
    for go in range(2):
        s = []
        for n, (u, g) in enumerate(quarters):
            ahead = maxima(*quarters[(n + LEAD) % len(quarters)])
            own = [[("score", u, g, c)] for c in range(chunks(u))]
            if n:
                v, h = quarters[n - 1]
                weighted = [[("pv", v, h, c)] for c in range(chunks(v))]
                weighted[-1] += [("ot", v)] if h == 3 else []
                own = [part for pair in zip_longest(own, weighted) for part in pair if part]
            own += [[x] for x in ready]
            ready = []
            other = []
            for part in fill[u, g]:
                if part[0][0] == "ff2":
                    other += [[("ff2_piece", part[0][1], i)] for i in range(FF2_PIECES - 1)]
                other.append(part)
            while own or ahead or other:
                for parts in (own, ahead, other):
                    if parts:
                        part = parts.pop(0)
                        s += part
                        if part[0][0] == "max_parts":
                            ready = [("mT",) + part[0][1:]]
    u = UNITS[-1]
    s += [("pv", u, 3, c) for c in range(chunks(u))] + [("ot", u), ("v1", 2), ("o1", u), ("v1", 3), ("o2", u), ("o3", u)]
    at = {t: i for i, t in enumerate(s)}

    def of_next(t):
        kind = t[0]
        if kind in ("load_tgt", "stats1", "norm1", "xT", "split_x", "qk1", "stack_q1", "stack_k1", "mask", "v1"):
            return True
        if kind in ("load_tb", "resid"):
            return t[1] == 0
        if kind in ("max", "max_parts", "mT", "score", "pv", "ot", "o1", "o2", "o3", "stats2", "norm2", "xq"):
            return t[1] in (0, 1) or (t[1] == UNITS[0] and kind in ("max", "max_parts", "mT") and at[t] > len(s) // 2)
        if kind in ("q2", "stack_q2"):
            return t[1] == 0
        if kind == "load_src":
            return t[1] < 3
        if kind in ("stats_s", "norm_s", "sT", "split_s", "k2", "stack_k2", "v2"):
            return t[1] in (0, 1) and at[t] > len(s) // 2
        return kind == "ff1" and at[t] > len(s) // 2

    return s, {t for t in s if of_next(t)}


class Order:

    def __init__(self, steps):
        self.steps = steps
        self.at = {s: i for i, s in enumerate(steps)}
        assert len(self.at) == len(steps)

    def of(self, *kinds):
        return [s for s in self.steps if s[0] in kinds]


def layer_kernel(nc, x, src, maskT, wqkv, sa_wproj, sa_bproj, ed_wkv, ed_wq, ed_wproj, ed_bproj,
                 ff_w1, ff_b1, ff_w2, ff_b2, g1, b1, g2, b2, g3, b3, out):
    B, T, C = x.shape
    S = src.shape[1]
    KT = C // P
    HD = C // H
    FT = ff_w1.shape[1] // P
    NT = BG * T
    SC = S // 3
    VW = HD + 1
    GH = 4
    SCALE = float(C) ** -0.5
    GROUPS = B // BG
    assert NT <= 512 and SC <= P and SC * 3 == S and GH * T <= 512 and FT == 4 * KT and H * HD == C
    NROW = SLOTS * HD
    SP2 = S + S % 2

    HH = H // 2
    NH = 2 * T

    steps, head = period_steps(KT)
    od = Order(steps)
    miscs = od.of(*MISC_READER)
    scores = od.of("score")
    maxes = od.of("max")
    splits = od.of("qk1", "k2", "q2")
    halves = od.of("mT")
    q_stacks = od.of("stack_q1", "stack_q2")
    k_stacks = od.of("stack_k1", "stack_k2")
    stacks = od.of("stack_q1", "stack_q2", "stack_k1", "stack_k2")
    LAND = 16 * SLOTS
    NORMS = {"stats1": (0, BG, T), "norm1": (0, BG, T), "stats_s": (1, 3, SC), "norm_s": (1, 3, SC),
             "stats2": (2, 1, T), "norm2": (2, 1, T)}

    K2_PLACE = (0, 1, 0, 1)
    K2_BEFORE = (BG + 2, BG + 3, BG, BG + 1)

    ff1_done = [t for t in od.of("ff1") if od.at[t] < od.at["ff2", 0]] or od.of("ff1")
    LAST_FF1 = ff1_done[-1]

    def unit_before(u):
        return UNITS[UNITS.index(u) - 1]

    def ran(R, step):
        return not isinstance(R, int) or (step in head) == (R == 0)

    def before_in(of_kind, step, size, R):
        n = of_kind.index(step)
        for m in range(n - size, -1, -size):
            if ran(R, of_kind[m]):
                return of_kind[m], False
        return of_kind[max(m for m in range(len(of_kind)) if m % size == n % size)], True

    with ExitStack() as ctx:
        def sb(name, shape, dt=F32):
            return ctx.enter_context(nc.sbuf_tensor(name, shape, dt))

        def ps(name, shape):
            return ctx.enter_context(nc.psum_tensor(name, shape, F32))

        def sem(name):
            return ctx.enter_context(nc.semaphore(name))

        wqk_hi = sb("wqk_hi", [P, KT, 2 * C], F32R)
        wqk_lo = sb("wqk_lo", [P, KT, 2 * C], F32R)
        wv1 = sb("wv1", [P, KT, C])
        wf1_hi = sb("wf1_hi", [P, KT, FT * P], F32R)
        wf1_lo = sb("wf1_lo", [P, KT, FT * P], F32R)
        wf2 = sb("wf2", [P, FT, C])
        wk2_hi = sb("wk2_hi", [P, KT, C], F32R)
        wk2_lo = sb("wk2_lo", [P, KT, C], F32R)
        wv2 = sb("wv2", [P, KT, C])
        wq2_hi = sb("wq2_hi", [P, KT, C], F32R)
        wq2_lo = sb("wq2_lo", [P, KT, C], F32R)
        wps = sb("wps", [P, KT, C])
        wpe = sb("wpe", [P, KT, C])
        gain = sb("gain", [P, 3, KT])
        offs = sb("offs", [P, 3, KT])
        bias1 = sb("bias1", [P, FT])
        NB = 2 * KT + KT + KT + FT
        bcol = sb("bcol", [P, NB])
        vb = sb("vb", [P, 2, KT])
        sab = sb("sab", [T, C])
        edb = sb("edb", [T, C])
        ident = sb("ident", [P, P])
        identb = sb("identb", [P, T], BF16)
        causal = sb("causal", [T, T])
        mhalf = sb("mhalf", [P, BG])
        epst = sb("epst", [P, BG])

        tb = sb("tb", [T, BG, C])
        xn = sb("xn", [T, BG, C])
        xr = sb("xr", [T, C])
        xq_hi = sb("xq_hi", [P, KT, NH], F32R)
        xq_lo = sb("xq_lo", [P, KT, NH], F32R)
        xT32 = sb("xT32", [P, KT, NT])
        xT_hi = sb("xT_hi", [P, KT, NT], F32R)
        xT_lo = sb("xT_lo", [P, KT, NT], F32R)
        hT = sb("hT", [P, FT, NT])
        qp = sb("qp", [P, KT, 3, NT], BF16)
        kp = sb("kp", [P, KT, 3, NT], BF16)
        rem = sb("rem", [P, NT])
        q1st = sb("q1st", [P, H, NT], BF16)
        q2st = sb("q2st", [P, H, NT], BF16)
        k1st = sb("k1st", [P, H, NT], BF16)
        k2flat = [sb(f"k2st{i}", [P, H * S], BF16) for i in range(2)]
        k2st = [f[:, :].rearrange("p (h s) -> p h s", h=H) for f in k2flat]
        v1 = sb("v1", [T, BG, H, VW])
        v2 = [sb(f"v2{i}", [SC, 3, H, VW]) for i in range(2)]
        xs = [sb(f"xs{i}", [SC, 3, C]) for i in range(2)]
        xsT32 = sb("xsT32", [P, KT, SP2])
        xsT_hi = sb("xsT_hi", [P, KT, SP2], F32R)
        xsT_lo = sb("xsT_lo", [P, KT, SP2], F32R)
        stats = sb("stats", [P, 3, BG, 6])
        mv = sb("mv", [P, 3, BG, 2])
        veps = sb("veps", [P, 3, BG])
        rstd = sb("rstd", [P, 3, BG])
        assert BG == 4
        mask8 = sb("mask8", [T, B], U8)
        pad = sb("pad", [T, B])
        padneg = sb("padneg", [T, BG])
        maskt = sb("maskt", [T, BG, T], BF16)
        negm = sb("negm", [T, 2, H])
        mrem = sb("mrem", [T, HH])
        mparts = [sb(f"mparts{i}", [T, 3, HH], BF16) for i in range(2)]
        mrows = [sb(f"mrows{i}", [3 * HH, T], BF16) for i in range(2)]
        prob = sb("prob", [P, PROB_SLOTS, GH * T])
        ot = sb("ot", [P, GH * T])
        rden = sb("rden", [T, H])
        att = sb("att", [T, H, HD])
        aT = sb("aT", [P, KT, T])
        ostage = sb("ostage", [T, C])

        hflat = hT[:, :, :].rearrange("p f n -> p (f n)")
        vbt = ot[:, 0:2 * KT * T].rearrange("p (a k t) -> p a k t", a=2, k=KT)
        edb2 = ostage[:, :]
        pflat = prob[:, :, :].rearrange("p s n -> p (s n)")
        raw_f1 = hflat[:, 0:KT * FT * P].rearrange("p (k n) -> p k n", k=KT)
        raw_qkv = hflat[:, KT * FT * P:KT * FT * P + KT * 3 * C].rearrange("p (k n) -> p k n", k=KT)
        raw_kv = pflat[:, 0:KT * 2 * C].rearrange("p (k n) -> p k n", k=KT)
        raw_q2 = pflat[:, KT * 2 * C:KT * 3 * C].rearrange("p (k n) -> p k n", k=KT)

        FOLDS = ((raw_qkv[:, :, 0:2 * C], 0, wqk_hi, wqk_lo), (raw_kv[:, :, 0:C], 1, wk2_hi, wk2_lo),
                 (raw_q2, 1, wq2_hi, wq2_lo), (raw_f1, 2, wf1_hi, wf1_lo))

        misc = [ps(f"misc{i}", [P, 512]) for i in range(MISC_BANKS)]
        mxb = [ps(f"mxb{i}", [P, 512]) for i in range(MAX_BANKS)]
        scb = [ps(f"scb{i}", [P, 512]) for i in range(SCORE_BANKS)]
        pvb = ps("pvb", [P, 512])
        qk_bank, vcol_bank, col_bank, row_bank, f1_bank = scb[0], scb[1], pvb, scb[0], scb[1]

        scr_q = nc.dram_tensor("scr_q", (KT, P, 3, NT), BF16).ap()
        scr_k1 = nc.dram_tensor("scr_k1", (KT, P, 3, NT), BF16).ap()
        scr_k2 = [nc.dram_tensor(f"scr_k2{i}", (KT, P, 3, S), BF16).ap() for i in range(2)]

        s_w = [sem(f"{w}_landed") for w in ("wqkv", "wkv", "wq2", "wff1")]
        s_wp = sem("output_projections_landed")
        s_wf2 = sem("wff2_landed")
        s_rowvec = sem("row_biases_landed")
        s_vec = sem("vectors_landed")
        s_const = sem("constants_made")
        s_init = sem("vector_constants_made")
        s_mqk = sem("qk_bias_columns_multiplied")
        s_mf1 = sem("hidden_bias_columns_multiplied")
        s_mcol = sem("bias_columns_multiplied")
        s_mvcol = sem("value_offsets_multiplied")
        s_mrow = sem("bias_rows_multiplied")
        s_vb = sem("value_offsets_made")
        s_fhi = sem("folded_hi_made")
        s_flo = sem("folded_lo_made")
        s_bcol = sem("bias_columns_made")
        s_vbt = sem("value_offsets_spread")
        s_rows = sem("bias_rows_made")
        s_xt = sem("tgt_landed")
        s_tb = [sem(f"residual_landed{h}") for h in range(2)]
        s_xh = sem("xq_hi_made")
        s_xs = [sem(f"src_landed{i}") for i in range(2)]
        s_pad = sem("pad_terms_made")
        s_mask = sem("mask_tile_made")
        s_bn = sem("row_stats_made")
        s_mv = sem("mean_var_made")
        s_ve = sem("var_plus_eps_made")
        s_rs = sem("rstd_made")
        s_norm = sem("rows_normalised")
        s_res = sem("residual_started")
        s_resb = sem("residual_has_cross_bias")
        s_full = sem("misc_bank_filled")
        s_read = {"act": sem("misc_bank_read_by_act"), "dve": sem("misc_bank_read_by_dve")}
        s_lo = sem("lo_made")
        s_p1 = sem("part1_made")
        s_p2 = sem("part2_made")
        s_p3 = sem("part3_made")
        s_step = sem("wait_holder")
        s_step_dve = sem("wait_holder_dve")
        s_scr = sem("parts_in_scratch")
        s_q1st = sem("q1_stack_landed")
        s_q2st = [sem(f"q2_stack_landed{h}") for h in range(2)]
        s_step_pool = sem("wait_holder_pool")
        s_k1st = sem("k1_stack_landed")
        s_k2st = [sem(f"k2_stack_landed{b}") for b in range(BG)]
        s_mxf = sem("max_scores_made")
        s_mx = sem("max_made")
        s_m1 = sem("max_part1_made")
        s_mrem = sem("max_remainder_made")
        s_m2 = sem("max_part2_made")
        s_m3 = sem("max_part3_made")
        s_neg = [sem(f"max_rows_landed{i}") for i in range(2)]
        s_sc = sem("scores_made")
        s_ex = sem("probs_made")
        s_pv = sem("values_weighted")
        s_ot = sem("weighted_copied")
        s_rd = sem("reciprocals_made")
        s_out = sem("output_stored")

        signals = {}

        def signalled(s, by, each=1):
            signals[id(s)] = (by, each)

        signalled(s_full, miscs)
        for e in ("act", "dve"):
            signalled(s_read[e], [t for t in miscs if MISC_READER[t[0]] == e])
        for s in (s_mxf, s_mx):
            signalled(s, maxes)
        for s in (s_sc, s_ex):
            signalled(s, scores)
        for s in (s_p1, s_p2, s_p3):
            signalled(s, splits)
        for s in (s_bn, s_mv, s_ve, s_rs):
            signalled(s, od.of("stats1", "stats_s", "stats2"))
        signalled(s_norm, od.of("norm1", "norm_s", "norm2"))
        signalled(s_lo, od.of("split_x", "split_s"))
        signalled(s_xh, od.of("xq"))
        for s in (s_m1, s_mrem, s_m2, s_m3):
            signalled(s, od.of("max_parts"))
        for i in range(2):
            signalled(s_neg[i], od.of("mT")[i::2], 16)
        signalled(s_pv, od.of("pv"))
        signalled(s_ot, od.of("ot"))
        signalled(s_rd, od.of("o1"))
        signalled(s_res, od.of("resid"))
        signalled(s_resb, od.of("norm2"))
        for s in (s_pad, s_mask):
            signalled(s, od.of("mask"))
        for b in range(BG):
            signalled(s_k2st[b], [("stack_k2", b)], LAND)
        signalled(s_xt, od.of("load_tgt"), 16)
        for h in range(2):
            signalled(s_tb[h], [("load_tb", h)], 16)
            signalled(s_q2st[h], [("stack_q2", h)], LAND)
        signalled(s_scr, stacks, 16 * KT)
        signalled(s_q1st, od.of("stack_q1"), LAND)
        signalled(s_out, [t for t in od.of("o3") if t[1] >= BG], 16)
        signalled(s_k1st, od.of("stack_k1"), LAND)
        for i in range(2):
            signalled(s_xs[i], [t for t in od.of("load_src") if t[1] % 2 == i], 16)

        def after(eng, R, now, s, step):
            by, each = signals[id(s)]
            step, earlier = step if isinstance(step[0], tuple) else (step, od.at[step] > od.at[now])
            n = by.index(step) + 1
            if isinstance(R, int) and R == 0:
                if step in head and not earlier:
                    eng.wait_ge(s, each * n)
            elif earlier:
                eng.wait_ge(s, R * (each * len(by)) - each * (len(by) - n))
            else:
                eng.wait_ge(s, R * (each * len(by)) + each * sum(ran(R, t) for t in by[:n]))

        def period_0(eng, part, sems):
            todo = list(steps)
            owed, real, count = {}, {}, {}

            def pay(s):
                if owed.get(id(s)):
                    if real.get(id(s)):
                        eng.wait_ge(s, count[id(s)])
                    eng.sem_inc(s, owed[id(s)])
                    count[id(s)] = count.get(id(s), 0) + owed[id(s)]
                    owed[id(s)], real[id(s)] = 0, False

            def run(last=None):
                while todo:
                    t = todo.pop(0)
                    for s in sems:
                        by, each = signals[id(s)]
                        if t in by and t in head:
                            pay(s)
                            real[id(s)] = True
                            count[id(s)] = count.get(id(s), 0) + each
                        elif t in by:
                            owed[id(s)] = owed.get(id(s), 0) + each
                    if t in head:
                        part(0, t)
                    if t == last:
                        return
                for s in sems:
                    pay(s)

            return run

        def period_0_done(eng, *sems):
            for s in sems:
                by, each = signals[id(s)]
                eng.wait_ge(s, each * len(by))

        def group_rows(R, s, b, n):
            if s in head:
                return bass.ds(R * BG + b, n)
            return bass.ds(R * BG - (BG - b), n)

        def split_of(R, step):
            kind, m = step[0], step[-1]
            if kind == "qk1" and m < KT:
                return qp[:, m], NT, m, before_in(q_stacks, ("stack_q1",), 1, R)
            if kind == "qk1":
                return kp[:, m - KT], NT, m, before_in(k_stacks, ("stack_k1",), 1, R)
            if kind == "q2":
                return qp[:, m], NH, 3 * KT + m, before_in(q_stacks, ("stack_q2", step[1]), 1, R)
            return kp[:, m], S, 2 * KT + m, before_in(k_stacks, ("stack_k2", step[1]), 1, R)

        def misc_bank(step):
            return misc[miscs.index(step) % MISC_BANKS]

        def wait_misc_free(pe, R, step):
            prev = before_in(miscs, step, MISC_BANKS, R)
            after(pe, R, step, s_read[MISC_READER[prev[0][0]]], prev)

        block = ctx.enter_context(nc.Block())

        @block.sync
        def _(sp):
            ctx.enter_context(nc.allow_non_contiguous_dma(reason="vectors by model dimension, mask bytes"))

            def w(dst, source, landed):
                sp.dma_start(dst, source.rearrange("(k p) n -> p k n", p=P)).then_inc(landed, 16)

            def v(dst, source):
                sp.dma_start(dst, source.rearrange("(k p) -> p k", p=P)).then_inc(s_vec, 16)

            def stack(R, s, parts, splits_of, scr, n, dst, part_of, landed, free=None):
                for m in range(KT):
                    after(sp, R, s, s_p3, splits_of[m])
                    sp.dma_start(scr[m, :, :, 0:n], parts[:, m, :, 0:n]).then_inc(s_scr, 16)
                after(sp, R, s, s_scr, s)
                if free is not None:
                    sp.sem_inc(s_step, 1)
                    after(sp, R, s, s_sc, free)
                for slot in range(SLOTS):
                    sp.dma_start(dst[HD * slot:HD * (slot + 1), :, 0:n],
                                 scr[:, :, part_of[slot], 0:n].rearrange("k (h d) t -> d (k h) t", d=HD)).then_inc(landed, 16)

            def transfers(R, s):
                kind = s[0]
                if kind == "load_tgt":
                    after(sp, R, s, s_full, ("xT", KT - 1))
                    sp.dma_start(xn[:, :, :], x[group_rows(R, s, 0, BG), :, :].rearrange("b t c -> t b c")).then_inc(s_xt, 16)
                elif kind == "load_tb":
                    h = s[1]
                    after(sp, R, s, s_read["dve"], ("o3", BG + 2 * h + 1))
                    sp.dma_start(tb[:, 2 * h:2 * h + 2, :], x[group_rows(R, s, 2 * h, 2), :, :].rearrange("b t c -> t b c")).then_inc(s_tb[h], 16)
                elif kind == "load_src":
                    b = s[1]
                    after(sp, R, s, s_full, ("sT", (b - 2) % BG, KT - 1))
                    sp.dma_start(xs[b % 2][:, :, :], src[group_rows(R, s, b, 1), :, :].rearrange("a (c s) n -> s (a c) n", c=3)).then_inc(s_xs[b % 2], 16)
                elif kind == "stack_q1":
                    stack(R, s, qp, [("qk1", m) for m in range(KT)], scr_q, NT, q1st, Q_PART, s_q1st, ("score", BG - 1, 3, 0))
                elif kind == "stack_k1":
                    stack(R, s, kp, [("qk1", KT + m) for m in range(KT)], scr_k1, NT, k1st, K_PART, s_k1st, ("score", BG - 1, 3, 0))
                elif kind == "stack_q2":
                    h = s[1]
                    stack(R, s, qp, [("q2", h, m) for m in range(KT)], scr_q, NH, q2st[:, :, h * NH:(h + 1) * NH], Q_PART, s_q2st[h],
                          ("score", BG + 2 * h + 1, 3, 2))
                elif kind == "stack_k2":
                    b = s[1]
                    stack(R, s, kp, [("k2", b, m) for m in range(KT)], scr_k2[b % 2], S, k2st[K2_PLACE[b]], K_PART, s_k2st[b],
                          ("score", K2_BEFORE[b], 3, chunks(K2_BEFORE[b]) - 1))
                elif kind == "o3" and s[1] >= BG:
                    b = s[1] - BG
                    after(sp, R, s, s_read["dve"], s)
                    sp.dma_start(out[group_rows(R, s, b, 1), :, :].rearrange("a t c -> t (a c)"), ostage[:, :]).then_inc(s_out, 16)

            start = period_0(sp, transfers, [s_xt, s_scr, s_q1st, s_k1st, s_out, *s_tb, *s_xs, *s_k2st, *s_q2st])
            start(("split_x",))
            w(raw_qkv, wqkv, s_w[0])
            for i, (g, b) in enumerate(((g1, b1), (g2, b2), (g3, b3))):
                v(gain[:, i, :], g)
                v(offs[:, i, :], b)
            v(bias1[:, :], ff_b1)
            sp.dma_start(mask8[:, :].bitcast(U32), maskT).then_inc(s_vec, 16)
            w(raw_kv, ed_wkv, s_w[1])
            w(raw_q2, ed_wq, s_w[2])
            w(raw_f1, ff_w1, s_w[3])
            w(wps[:, :, :], sa_wproj, s_wp)
            w(wpe[:, :, :], ed_wproj, s_wp)
            for dst, vec in ((sab[:, :], sa_bproj), (edb[:, :], ed_bproj), (edb2, ff_b2)):
                sp.dma_start(dst, vec.rearrange("(a n) -> a n", a=1).broadcast_to([T, C])).then_inc(s_rowvec, 16)
            w(wf2[:, :, :], ff_w2, s_wf2)
            start()
            period_0_done(sp, s_full)
            with sp.Fori(1, GROUPS) as R:
                for s in steps:
                    transfers(R, s)
            for s in steps:
                if s not in head:
                    transfers(GROUPS, s)
            sp.wait_ge(s_out, 16 * BG * (GROUPS + 1))

        @block.gpsimd
        def _(pool):
            nc.gpsimd.memset(ident[:, :], 0.0).then_inc(s_const, 1)
            nc.gpsimd.memset(causal[:, :], 0.0).then_inc(s_const, 1)
            nc.gpsimd.memset(mhalf[:, :], -0.5).then_inc(s_const, 1)
            nc.gpsimd.memset(epst[:, :], EPS).then_inc(s_const, 1)
            pool.wait_ge(s_const, 4)
            nc.gpsimd.affine_select(out=ident[:, :], in_=ident[:, :], compare_op=ALU.not_equal, fill=1.0,
                                    base=0, pattern=[[-1, P]], channel_multiplier=1).then_inc(s_const, 1)
            nc.gpsimd.affine_select(out=causal[:, :], in_=causal[:, :], compare_op=ALU.is_ge, fill=MASKED,
                                    base=0, pattern=[[1, T]], channel_multiplier=-1).then_inc(s_const, 1)
            def pool_part(R, s):
                kind = s[0]
                if kind in NORMS and kind.startswith("stats"):
                    w, n, rows = NORMS[kind]
                    after(pool, R, s, s_mv, s)
                    nc.gpsimd.tensor_tensor(veps[0:rows, w, 0:n], mv[0:rows, w, 0:n, 1], epst[0:rows, 0:n], ALU.add).then_inc(s_ve, 1)
                    after(pool, R, s, s_ve, s)
                    nc.gpsimd.tensor_tensor(rstd[0:rows, w, 0:n], veps[0:rows, w, 0:n], mhalf[0:rows, 0:n], ALU.pow).then_inc(s_rs, 1)
                elif kind == "norm2":
                    b = s[1]
                    after(pool, R, s, s_norm, s)
                    nc.gpsimd.tensor_tensor(tb[:, b, :], tb[:, b, :], edb[:, :], ALU.add).then_inc(s_resb, 1)
                elif kind == "resid":
                    h = s[1]
                    after(pool, R, s, s_tb[h], ("load_tb", h))
                    nc.gpsimd.tensor_tensor(tb[:, 2 * h:2 * h + 2, :], tb[:, 2 * h:2 * h + 2, :],
                                            sab[:, :].unsqueeze(1).broadcast_to([T, 2, C]), ALU.add).then_inc(s_res, 1)
                elif kind == "max_parts":
                    u, half = s[1:]
                    n = halves.index(("mT", u, half))
                    neg = negm[:, u % 2, half * HH:(half + 1) * HH]
                    parts = mparts[n % 2]
                    after(pool, R, s, s_mx, ("max", u, 2 * half + 1 if u < BG else (half + 1) * HH - 1))
                    after(pool, R, s, s_full, before_in(halves, ("mT", u, half), 2, R))
                    pool.sem_inc(s_step_pool, 1)
                    nc.gpsimd.tensor_copy(parts[:, 0, :], neg).then_inc(s_m1, 1)
                    after(pool, R, s, s_m1, s)
                    nc.gpsimd.tensor_tensor(mrem[:, :], neg, parts[:, 0, :], ALU.subtract).then_inc(s_mrem, 1)
                    after(pool, R, s, s_mrem, s)
                    pool.sem_inc(s_step_pool, 1)
                    nc.gpsimd.tensor_copy(parts[:, 1, :], mrem[:, :]).then_inc(s_m2, 1)
                    after(pool, R, s, s_m2, s)
                    nc.gpsimd.tensor_tensor(parts[:, 2, :], mrem[:, :], parts[:, 1, :], ALU.subtract).then_inc(s_m3, 1)

            start = period_0(pool, pool_part, [s_ve, s_rs, s_m1, s_mrem, s_m2, s_m3, s_res, s_resb])
            start(("split_x",))
            after(pool, 0, ("norm1",), s_rs, ("stats1",))
            stack_rows = [k1st[NROW:, :, :], k2st[0][NROW:, :, :], k2st[1][NROW:, :, :]]
            for i, (flat, rows) in enumerate(zip((k1st[NROW:, :, :], k2flat[0][NROW:, :], k2flat[1][NROW:, :]), stack_rows)):
                pool.wait_ge(s_const, 6 + 2 * i)
                nc.gpsimd.memset(flat.bitcast(F32), 0.0).then_inc(s_const, 1)
                pool.wait_ge(s_const, 7 + 2 * i)
                nc.gpsimd.memset(rows[0:3], 1.0).then_inc(s_const, 1)
            pool.wait_ge(s_const, 12)
            start(("max_parts", 0, 1))
            pool.wait_ge(s_rows, 2)
            start()
            period_0_done(pool, s_full)
            with pool.Fori(1, GROUPS) as R:
                for s in steps:
                    pool_part(R, s)
            for s in steps:
                if s not in head:
                    pool_part(GROUPS, s)

        @block.scalar
        def _(act):

            def act_part(R, s):
                kind = s[0]
                if MISC_READER.get(kind) == "act":
                    after(act, R, s, s_full, s)
                    bank = misc_bank(s)
                if kind == "xT":
                    k = s[1]
                    after(act, R, s, s_lo, ("split_x",))
                    nc.scalar.activation(xT32[:, k, :], bank[:, 0:NT], ACT.Copy)
                    nc.scalar.activation(xT_hi[:, k, :], bank[:, 0:NT], ACT.Copy).then_inc(s_read["act"], 1)
                elif kind == "xq":
                    b = s[1]
                    after(act, R, s, s_full, s)
                    nc.scalar.activation(xq_hi[:, :, b % 2 * T:(b % 2 + 1) * T], misc_bank(s)[:, 0:KT * T].rearrange("p (k t) -> p k t", k=KT), ACT.Copy).then_inc(s_xh, 1)
                elif kind == "sT":
                    b, k = s[1:]
                    after(act, R, s, s_lo, ("split_s", (b - 1) % BG))
                    nc.scalar.activation(xsT32[:, k, 0:S], bank[:, 0:S], ACT.Copy)
                    nc.scalar.activation(xsT_hi[:, k, 0:S], bank[:, 0:S], ACT.Copy).then_inc(s_read["act"], 1)
                elif kind == "ff1":
                    m = s[1]
                    nc.scalar.activation(hT[:, m, :], bank[:, 0:NT], ACT.Relu, bias=bcol[:, 4 * KT + m:4 * KT + m + 1]).then_inc(s_read["act"], 1)
                elif kind == "v1":
                    b = s[1]
                    after(act, R, s, s_pv, ("pv", b, 3, 0))
                    nc.scalar.activation(v1[0:T, b, :, 0:HD], bank[0:T, 0:C].rearrange("p (h d) -> p h d", h=H), ACT.Copy).then_inc(s_read["act"], 1)
                elif kind == "v2":
                    b, c = s[1:]
                    after(act, R, s, s_pv, ("pv", K2_BEFORE[b], 3, 2))
                    nc.scalar.activation(v2[K2_PLACE[b]][0:SC, c, :, 0:HD], bank[0:SC, 0:C].rearrange("p (h d) -> p h d", h=H), ACT.Copy).then_inc(s_read["act"], 1)
                elif kind in ("qk1", "q2", "k2"):
                    parts, n, col, stack = split_of(R, s)
                    after(act, R, s, s_full, s)
                    after(act, R, s, s_scr, stack)
                    nc.scalar.activation(parts[:, 0, 0:n], misc_bank(s)[:, 0:n], ACT.Identity, bias=bcol[:, col:col + 1]).then_inc(s_p1, 1)
                elif kind == "mT":
                    u, half = s[1:]
                    n = halves.index(s)
                    b = u % BG
                    after(act, R, s, s_neg[n % 2], before_in(halves, s, 2, R))
                    nc.scalar.activation(mrows[n % 2][:, :], bank[0:3 * HH, 0:T], ACT.Copy).then_inc(s_read["act"], 1)
                    after(act, R, s, s_read["act"], s)
                    act.dma_start((q1st if u < BG else q2st)[NROW:NROW + 3, half * HH:(half + 1) * HH, b * T:(b + 1) * T], mrows[n % 2][:, :]).then_inc(s_neg[n % 2], 16)
                elif kind == "o2":
                    u = s[1]
                    nc.scalar.activation(aT[:, :, :], bank[:, 0:KT * T].rearrange("p (k t) -> p k t", k=KT), ACT.Copy).then_inc(s_read["act"], 1)
                elif kind == "score":
                    n = scores.index(s)
                    rows = T if s[1] < BG else SC
                    after(act, R, s, s_sc, s)
                    old, earlier = before_in(scores, s, PROB_SLOTS, R)
                    after(act, R, s, s_pv, (("pv",) + old[1:], earlier))
                    nc.scalar.activation(prob[0:rows, n % PROB_SLOTS, :], scb[n % SCORE_BANKS][0:rows, 0:GH * T], ACT.Exp,
                                         scale=SCALE).then_inc(s_ex, 1)
                elif kind == "ot":
                    u = s[1]
                    after(act, R, s, s_pv, ("pv", u, 3, chunks(u) - 1))
                    after(act, R, s, s_full, ("o1", unit_before(u)))
                    nc.scalar.activation(ot[:, :], pvb[:, 0:GH * T], ACT.Copy).then_inc(s_ot, 1)

            start = period_0(act, act_part, [s_read["act"], s_ex, s_ot, s_p1, s_xh, *s_neg])
            start(("split_x",))
            act.wait_ge(s_vec, 128)
            def fold(dst, raw, k, i):
                nc.scalar.activation(dst[:, k, :], raw[:, k, :], ACT.Copy, scale=gain[:, i, k:k + 1]).then_inc(s_fhi, 1)

            for n, (raw, i, hi, lo) in enumerate(FOLDS):
                act.wait_ge(s_w[n], 16)
                for k in range(KT):
                    fold(hi, raw, k, i)
                if n == 0:
                    for k in range(KT):
                        fold(wv1, raw_qkv[:, :, 2 * C:3 * C], k, 0)
                    act.wait_ge(s_bcol, 1)
                    start(("qk1", 2 * KT - 1))
            for k in range(KT):
                fold(wv2, raw_kv[:, :, C:2 * C], k, 1)
            act.wait_ge(s_bcol, 2)
            act.wait_ge(s_bcol, 3)
            start()
            period_0_done(act, s_full, s_pv, s_neg[0], s_neg[1])
            with act.Fori(1, GROUPS) as R:
                for s in steps:
                    act_part(R, s)
            for s in steps:
                if s not in head:
                    act_part(GROUPS, s)

        @block.vector
        def _(dve):
            V = nc.vector
            def row_stats(R, s, row_set):
                w, n, rows = NORMS[s[0]]
                for j in range(n):
                    i = V.bn_stats(stats[0:rows, w, j, :], row_set(j))
                i.then_inc(s_bn, 1)
                after(dve, R, s, s_bn, s)
                dve.sem_inc(s_step_dve, 1)
                for j in range(n):
                    i = V.bn_aggr(mv[0:rows, w, j, :], stats[0:rows, w, j, :])
                i.then_inc(s_mv, 1)

            def normalise(R, s, stats_step, from_set, to_set):
                w, n, rows = NORMS[s[0]]
                after(dve, R, s, s_rs, stats_step)
                for j in range(n):
                    i = V.tensor_scalar(to_set(j), from_set(j), mv[0:rows, w, j, 0:1], rstd[0:rows, w, j:j + 1], ALU.subtract, ALU.mult)
                i.then_inc(s_norm, 1)

            def lo_part(x32, hi, lo):
                V.tensor_tensor(lo, x32, hi.bitcast(F32), ALU.subtract).then_inc(s_lo, 1)

            def split3(R, s, bank, n, bias, parts, r):
                after(dve, R, s, s_p3, before_in(splits, s, 1, R))
                after(dve, R, s, s_p1, s)
                V.scalar_tensor_tensor(r[:, 0:n], bank[:, 0:n], bias, parts[:, 0, 0:n], ALU.add, ALU.subtract).then_inc(s_read["dve"], 1)
                after(dve, R, s, s_read["dve"], s)
                V.tensor_copy(parts[:, 1, 0:n], r[:, 0:n]).then_inc(s_p2, 1)
                after(dve, R, s, s_p2, s)
                V.tensor_tensor(parts[:, 2, 0:n], r[:, 0:n], parts[:, 1, 0:n], ALU.subtract).then_inc(s_p3, 1)

            def dve_part(R, s):
                kind = s[0]
                if MISC_READER.get(kind) == "dve":
                    if kind not in ("qk1", "k2", "q2", "xq"):
                        after(dve, R, s, s_full, s)
                    bank = misc_bank(s)
                if kind == "mask":
                    V.tensor_copy(padneg[:, :], pad[:, bass.ds(R * BG, BG)]).then_inc(s_pad, 1)
                    after(dve, R, s, s_pad, s)
                    after(dve, R, s, s_sc, ("score", BG - 1, 3, 0))
                    for b in range(BG):
                        i = V.tensor_scalar(maskt[:, b, :], causal[:, :], padneg[:, b:b + 1], None, ALU.add)
                    i.then_inc(s_mask, 1)
                elif kind == "stats1":
                    after(dve, R, s, s_xt, ("load_tgt",))
                    row_stats(R, s, lambda j: xn[:, j, :])
                elif kind == "norm1":
                    normalise(R, s, ("stats1",), lambda j: xn[:, j, :], lambda j: xn[:, j, :])
                elif kind == "stats_s":
                    b = s[1]
                    after(dve, R, s, s_xs[b % 2], ("load_src", b))
                    row_stats(R, s, lambda j: xs[b % 2][:, j, :])
                elif kind == "norm_s":
                    b = s[1]
                    normalise(R, s, ("stats_s", b), lambda j: xs[b % 2][:, j, :], lambda j: xs[b % 2][:, j, :])
                elif kind == "stats2":
                    b = s[1]
                    after(dve, R, s, s_read["dve"], ("o3", b))
                    row_stats(R, s, lambda j: tb[:, b, :])
                elif kind == "norm2":
                    b = s[1]
                    prev, earlier = before_in(od.of("xq"), ("xq", b), 1, R)
                    after(dve, R, s, s_full, (prev, earlier))
                    normalise(R, s, ("stats2", b), lambda j: tb[:, b, :], lambda j: xr[:, :])
                elif kind == "split_x":
                    after(dve, R, s, s_read["act"], ("xT", KT - 1))
                    lo_part(xT32[:, :, :], xT_hi[:, :, :], xT_lo[:, :, :])
                elif kind == "split_s":
                    b = s[1]
                    after(dve, R, s, s_read["act"], ("sT", b, KT - 1))
                    lo_part(xsT32[:, :, :], xsT_hi[:, :, :], xsT_lo[:, :, :])
                elif kind == "xq":
                    b = s[1]
                    after(dve, R, s, s_xh, s)
                    c = slice(b % 2 * T, (b % 2 + 1) * T)
                    V.tensor_tensor(xq_lo[:, :, c], bank[:, 0:KT * T].rearrange("p (k t) -> p k t", k=KT), xq_hi[:, :, c].bitcast(F32),
                                    ALU.subtract).then_inc(s_read["dve"], 1)
                elif kind in ("qk1", "q2", "k2"):
                    parts, n, col, _ = split_of(R, s)
                    split3(R, s, bank, n, bcol[:, col:col + 1], parts, rem)
                elif kind == "max":
                    u, i = s[1:]
                    mx = mxb[maxes.index(s) % MAX_BANKS]
                    after(dve, R, s, s_mxf, s)
                    if i == 0:
                        after(dve, R, s, s_m3, before_in([t for t in od.of("max_parts") if t[2]], ("max_parts", u, 1), 2, R))
                    if u < BG:
                        V.tensor_reduce(negm[:, u % 2, i * GH:(i + 1) * GH], mx[0:T, 0:GH * T].rearrange("p (h s) -> p h s", h=GH),
                                        axis=AX_X, op=ALU.max, negate=True).then_inc(s_mx, 1)
                    else:
                        V.tensor_reduce(negm[:, u % 2, i:i + 1], mx[0:T, 0:S],
                                        axis=AX_X, op=ALU.max, negate=True).then_inc(s_mx, 1)
                elif kind == "o1":
                    u = s[1]
                    heads = bank[0:T, :].rearrange("p (h x) -> p h x", h=H)
                    V.reciprocal(rden[:, :], heads[:, :, HD]).then_inc(s_rd, 1)
                    after(dve, R, s, s_rd, s)
                    V.tensor_tensor(att[:, :, :], heads[:, :, 0:HD], rden[:, :].unsqueeze(2).broadcast_to([T, H, HD]),
                                    ALU.mult).then_inc(s_read["dve"], 1)
                elif kind == "ff2":
                    b = s[1]
                    after(dve, R, s, s_resb, ("norm2", b))
                    V.tensor_tensor(tb[:, b, :], bank[0:T, 0:C], tb[:, b, :], ALU.add).then_inc(s_read["dve"], 1)
                elif kind == "o3":
                    u = s[1]
                    b = u % BG
                    if u < BG:
                        after(dve, R, s, s_res, ("resid", b // 2))
                        V.tensor_tensor(tb[:, b, :], bank[0:T, 0:C], tb[:, b, :], ALU.add).then_inc(s_read["dve"], 1)
                    else:
                        after(dve, R, s, s_read["dve"], ("ff2", b))
                        after(dve, R, s, s_out, ("o3", BG + (b - 1) % BG))
                        V.tensor_tensor(ostage[:, :], bank[0:T, 0:C], tb[:, b, :], ALU.add).then_inc(s_read["dve"], 1)
            V.memset(q1st[NROW:P, :, :].bitcast(F32), 0.0).then_inc(s_init, 1)
            start = period_0(dve, dve_part, [s_read["dve"], s_p2, s_p3, s_bn, s_mv, s_norm, s_lo, s_mx, s_rd, s_pad, s_mask])
            start(("split_x",))
            V.memset(xsT32[:, :, :], 0.0).then_inc(s_init, 1)
            V.memset(xsT_hi[:, :, :].bitcast(F32), 0.0).then_inc(s_init, 1)
            dve.wait_ge(s_const, 6)
            V.tensor_copy(identb[0:T, :], ident[0:T, 0:T]).then_inc(s_init, 1)
            dve.wait_ge(s_vec, 128)

            def lo_of(n, seen):
                raw, i, hi, lo = FOLDS[n]
                for k in range(KT):
                    dve.wait_ge(s_fhi, seen + k + 1)
                    V.scalar_tensor_tensor(lo[:, k, :], raw[:, k, :], gain[:, i, k:k + 1], hi[:, k, :].bitcast(F32), ALU.mult, ALU.subtract).then_inc(s_flo, 1)

            lo_of(0, 0)
            V.tensor_scalar(pad[:, :], mask8[:, :], MASKED, None, ALU.mult).then_inc(s_init, 1)
            dve.wait_ge(s_mqk, 1)
            V.tensor_copy(bcol[:, 0:2 * KT], qk_bank[:, 0:2 * KT]).then_inc(s_bcol, 1)
            start(("mask",))
            V.memset(v1[:, :, :, HD:VW], 1.0).then_inc(s_init, 1)
            for i in range(2):
                V.memset(v2[i][:, :, :, HD:VW], 1.0).then_inc(s_init, 1)
            dve.wait_ge(s_mvcol, 1)
            V.tensor_copy(vb[:, :, :], vcol_bank[:, 0:2 * KT].rearrange("p (a k) -> p a k", a=2)).then_inc(s_vb, 1)
            dve.wait_ge(s_vb, 1)
            V.tensor_copy(vbt[:, :, :, :], vb[:, :, :].unsqueeze(3).broadcast_to([P, 2, KT, T])).then_inc(s_vbt, 1)
            dve.wait_ge(s_mcol, 1)
            V.tensor_copy(bcol[:, 2 * KT:4 * KT], col_bank[:, 2 * KT:4 * KT]).then_inc(s_bcol, 1)
            for n in range(1, 4):
                lo_of(n, (n + 1) * KT)
            V.memset(q2st[NROW:P, :, :].bitcast(F32), 0.0).then_inc(s_init, 1)
            dve.wait_ge(s_bcol, 2)
            V.memset(pvb[:, :], 0.0).then_inc(s_init, 1)
            dve.wait_ge(s_rowvec, 48)
            V.tensor_tensor(edb[:, :], edb[:, :], edb2, ALU.add).then_inc(s_init, 1)
            dve.wait_ge(s_mf1, 1)
            V.tensor_tensor(bcol[:, 4 * KT:NB], f1_bank[:, 0:FT], bias1[:, :], ALU.add).then_inc(s_bcol, 1)
            dve.wait_ge(s_mrow, 1)
            dve.wait_ge(s_init, 11)
            V.tensor_tensor(sab[:, :], row_bank[0:T, 0:C], sab[:, :], ALU.add).then_inc(s_rows, 1)
            V.tensor_tensor(edb[:, :], row_bank[0:T, C:2 * C], edb[:, :], ALU.add).then_inc(s_rows, 1)
            start()
            period_0_done(dve, s_m3, s_full)
            with dve.Fori(1, GROUPS) as R:
                for s in steps:
                    dve_part(R, s)
            for s in steps:
                if s not in head:
                    dve_part(GROUPS, s)

        @block.tensor
        def _(pe):
            M = nc.tensor.matmul
            def three_pass(dst, w_hi, w_lo, x_hi, x_lo):
                for k in range(KT):
                    M(dst, w_hi[:, k], x_hi[:, k], start=(k == 0), stop=False)
                    M(dst, w_hi[:, k], x_lo[:, k], start=False, stop=False)
                    mm = M(dst, w_lo[:, k], x_hi[:, k], start=False, stop=(k == KT - 1))
                return mm

            def plain(dst, xx, w):
                for k in range(KT):
                    mm = M(dst, xx[:, k], w[:, k], start=(k == 0), stop=(k == KT - 1))
                return mm

            def pe_part(R, s):
                kind = s[0]
                if kind in MISC_READER and kind != "ff2":
                    wait_misc_free(pe, R, s)
                    bank = misc_bank(s)
                if kind == "xT":
                    k = s[1]
                    after(pe, R, s, s_norm, ("norm1",))
                    for b in range(BG):
                        mm = nc.tensor.transpose(bank[:, b * T:(b + 1) * T], xn[:, b, k * P:(k + 1) * P], ident[0:T, 0:T])
                    mm.then_inc(s_full, 1)
                elif kind == "qk1":
                    m = s[1]
                    after(pe, R, s, s_lo, ("split_x",))
                    c = slice(m * P, (m + 1) * P)
                    three_pass(bank[:, 0:NT], wqk_hi[:, :, c], wqk_lo[:, :, c], xT_hi, xT_lo).then_inc(s_full, 1)
                elif kind == "v1":
                    b = s[1]
                    after(pe, R, s, s_read["act"], ("xT", KT - 1))
                    plain(bank[0:T, 0:C], xT32[:, :, b * T:(b + 1) * T], wv1).then_inc(s_full, 1)
                elif kind == "ff1":
                    m = s[1]
                    c = slice(m * P, (m + 1) * P)
                    three_pass(bank[:, 0:NT], wf1_hi[:, :, c], wf1_lo[:, :, c], xT_hi, xT_lo).then_inc(s_full, 1)
                elif kind == "sT":
                    b, k = s[1:]
                    after(pe, R, s, s_norm, ("norm_s", b))
                    for c in range(3):
                        mm = nc.tensor.transpose(bank[:, c * SC:(c + 1) * SC], xs[b % 2][:, c, k * P:(k + 1) * P], ident[0:SC, 0:SC])
                    mm.then_inc(s_full, 1)
                elif kind == "k2":
                    b, m = s[1:]
                    after(pe, R, s, s_lo, ("split_s", b))
                    c = slice(m * P, (m + 1) * P)
                    three_pass(bank[:, 0:SP2], wk2_hi[:, :, c], wk2_lo[:, :, c], xsT_hi, xsT_lo).then_inc(s_full, 1)
                elif kind == "v2":
                    b, c = s[1:]
                    after(pe, R, s, s_read["act"], ("sT", b, KT - 1))
                    plain(bank[0:SC, 0:C], xsT32[:, :, c * SC:(c + 1) * SC], wv2).then_inc(s_full, 1)
                elif kind == "xq":
                    b = s[1]
                    after(pe, R, s, s_norm, ("norm2", b))
                    for k in range(KT):
                        mm = nc.tensor.transpose(bank[:, k * T:(k + 1) * T], xr[:, k * P:(k + 1) * P], ident[0:T, 0:T])
                    mm.then_inc(s_full, 1)
                elif kind == "q2":
                    h, m = s[1:]
                    after(pe, R, s, s_read["dve"], ("xq", 2 * h + 1))
                    c = slice(m * P, (m + 1) * P)
                    three_pass(bank[:, 0:NH], wq2_hi[:, :, c], wq2_lo[:, :, c], xq_hi, xq_lo).then_inc(s_full, 1)
                elif kind == "max":
                    u, i = s[1:]
                    mx = mxb[maxes.index(s) % MAX_BANKS]
                    b = u % BG
                    after(pe, R, s, s_mx, before_in(maxes, s, MAX_BANKS, R))
                    if i == 0 and u < BG:
                        after(pe, R, s, s_mask, ("mask",))
                        after(pe, R, s, s_q1st, ("stack_q1",))
                        after(pe, R, s, s_k1st, ("stack_k1",))
                    elif i == 0:
                        after(pe, R, s, s_q2st[b // 2], ("stack_q2", b // 2))
                        after(pe, R, s, s_k2st[b], ("stack_k2", b))
                    if u < BG:
                        M(mx[0:T, 0:GH * T].rearrange("p (h s) -> p h s", h=GH), maskt[:, b, :],
                          identb[0:T, :].unsqueeze(1).broadcast_to([T, GH, T]), start=True, stop=False)
                        for j in range(GH):
                            h = i * GH + j
                            mm = M(mx[0:T, j * T:(j + 1) * T], q1st[0:NROW, h, b * T:(b + 1) * T], k1st[0:NROW, h, b * T:(b + 1) * T],
                                   start=False, stop=(j == GH - 1))
                    else:
                        mm = M(mx[0:T, 0:S], q2st[0:NROW, i, b * T:(b + 1) * T], k2st[K2_PLACE[b]][0:NROW, i, 0:S], start=True, stop=True)
                    mm.then_inc(s_mxf, 1)
                elif kind == "score":
                    u, g, c = s[1:]
                    b = u % BG
                    rows = T if u < BG else SC
                    sc = scb[scores.index(s) % SCORE_BANKS]
                    after(pe, R, s, s_ex, before_in(scores, s, SCORE_BANKS, R))
                    after(pe, R, s, s_neg[halves.index(("mT", u, g // 2)) % 2], ("mT", u, g // 2))
                    if u < BG:
                        M(sc[0:T, 0:GH * T].rearrange("p (h t) -> p h t", h=GH), identb[0:T, :],
                          maskt[:, b, :].unsqueeze(1).broadcast_to([T, GH, T]), start=True, stop=False)
                    for j in range(GH):
                        h = g * GH + j
                        ks = k1st[:, h, b * T:(b + 1) * T] if u < BG else k2st[K2_PLACE[b]][:, h, c * SC:(c + 1) * SC]
                        mm = M(sc[0:rows, j * T:(j + 1) * T], ks, (q1st if u < BG else q2st)[:, h, b * T:(b + 1) * T], start=(u >= BG), stop=(u >= BG or j == GH - 1))
                    mm.then_inc(s_sc, 1)
                elif kind == "pv":
                    u, g, c = s[1:]
                    b = u % BG
                    if g == 0 and c == 0:
                        after(pe, R, s, s_ot, ("ot", unit_before(u)))
                    after(pe, R, s, s_read["act"], ("v1", b) if u < BG else ("v2", b, 2))
                    after(pe, R, s, s_ex, ("score", u, g, c))
                    slot = scores.index(("score", u, g, c)) % PROB_SLOTS
                    rows = T if u < BG else SC
                    for j in range(GH):
                        h = g * GH + j
                        vals = v1[0:T, b, h, :] if u < BG else v2[K2_PLACE[b]][0:SC, c, h, :]
                        mm = M(pvb[32 * j:32 * j + VW, g * T:(g + 1) * T], vals,
                               prob[0:rows, slot, j * T:(j + 1) * T], start=(c == 0), stop=(c == chunks(u) - 1))
                    mm.then_inc(s_pv, 1)
                elif kind == "o1":
                    u = s[1]
                    after(pe, R, s, s_ot, ("ot", u))
                    for g in range(4):
                        mm = nc.tensor.transpose(bank[0:T, g * P:(g + 1) * P], ot[:, g * T:(g + 1) * T], ident[:, :])
                    mm.then_inc(s_full, 1)
                elif kind == "mT":
                    u, half = s[1:]
                    after(pe, R, s, s_m3, ("max_parts", u, half))
                    M(bank[0:3 * HH, 0:T], mparts[halves.index(s) % 2][:, :, :].rearrange("p a h -> p (a h)"), identb[0:T, :],
                      start=True, stop=True).then_inc(s_full, 1)
                elif kind == "o2":
                    u = s[1]
                    after(pe, R, s, s_read["dve"], ("o1", u))
                    for k in range(KT):
                        mm = nc.tensor.transpose(bank[:, k * T:(k + 1) * T], att[:, :, :].rearrange("p h d -> p (h d)")[:, k * P:(k + 1) * P], ident[0:T, 0:T])
                    mm.then_inc(s_full, 1)
                elif kind in ("ff2_piece", "ff2"):
                    b = s[1]
                    i = s[2] if kind == "ff2_piece" else FF2_PIECES - 1
                    bank = misc_bank(("ff2", b))
                    if i == 0:
                        assert od.at[before_in(miscs, ("ff2", b), MISC_BANKS, 1)[0]] < od.at[s]
                        wait_misc_free(pe, R, ("ff2", b))
                        after(pe, R, s, s_read["act"], LAST_FF1)
                    for f in range(i * FT // FF2_PIECES, (i + 1) * FT // FF2_PIECES):
                        mm = M(bank[0:T, 0:C], hT[:, f, b * T:(b + 1) * T], wf2[:, f, :], start=(f == 0), stop=(f == FT - 1))
                    if i == FF2_PIECES - 1:
                        mm.then_inc(s_full, 1)
                elif kind == "o3":
                    u = s[1]
                    after(pe, R, s, s_read["act"], ("o2", u))
                    for k in range(KT):
                        mm = M(bank[0:T, 0:C], aT[:, k, :], (wps, wpe)[u // BG][:, k, :], start=(k == 0), stop=(k == KT - 1))
                    mm.then_inc(s_full, 1)
            def bias_columns(bank, cols):
                for n, raw, c0, i in cols:
                    for k in range(KT):
                        mm = M(bank[:, n:n + 1], raw[:, k, c0:c0 + P], offs[:, i, k:k + 1], start=(k == 0), stop=(k == KT - 1))
                return mm

            pe.wait_ge(s_vec, 128)
            pe.wait_ge(s_w[0], 16)
            bias_columns(qk_bank, [(m, raw_qkv, m * P, 0) for m in range(2 * KT)]).then_inc(s_mqk, 1)
            pe.wait_ge(s_const, 6)
            start = period_0(pe, pe_part, [s_full, s_mxf, s_sc, s_pv])
            start(("split_x",))
            pe.wait_ge(s_fhi, 2 * KT)
            pe.wait_ge(s_flo, KT)
            start(("qk1", 2 * KT - 1))
            bias_columns(vcol_bank, [(m, raw_qkv, 2 * C + m * P, 0) for m in range(KT)])
            pe.wait_ge(s_w[1], 16)
            bias_columns(vcol_bank, [(KT + m, raw_kv, C + m * P, 1) for m in range(KT)]).then_inc(s_mvcol, 1)
            bias_columns(col_bank, [(2 * KT + m, raw_kv, m * P, 1) for m in range(KT)])
            pe.wait_ge(s_w[2], 16)
            mm = bias_columns(col_bank, [(3 * KT + m, raw_q2, m * P, 1) for m in range(KT)])
            mm.then_inc(s_mcol, 1)
            pe.wait_ge(s_vbt, 1)
            pe.wait_ge(s_w[3], 16)
            bias_columns(f1_bank, [(m, raw_f1, m * P, 2) for m in range(FT)]).then_inc(s_mf1, 1)
            pe.wait_ge(s_wp, 32)
            for a, w in ((0, wps), (1, wpe)):
                for k in range(KT):
                    mm = M(row_bank[0:T, a * C:(a + 1) * C], vbt[:, a, k, :], w[:, k, :], start=(k == 0), stop=(k == KT - 1))
            mm.then_inc(s_mrow, 1)
            pe.wait_ge(s_const, 8)
            pe.wait_ge(s_init, 4)
            pe.wait_ge(s_fhi, 6 * KT)
            pe.wait_ge(s_wf2, 16)
            pe.wait_ge(s_flo, 4 * KT)
            pe.wait_ge(s_init, 11)
            pe.wait_ge(s_rows, 2)
            pe.wait_ge(s_bcol, 3)

            start()
            pe.wait_ge(s_const, 12)
            period_0_done(pe, s_read["act"], s_read["dve"], s_ex, s_mx, s_ot)
            with pe.Fori(1, GROUPS) as R:
                for s in steps:
                    pe_part(R, s)
            for s in steps:
                if s not in head:
                    pe_part(GROUPS, s)


_WEIGHTS = ["sa_wqkv", "sa_wproj", "sa_bproj", "ed_wkv", "ed_wq", "ed_wproj", "ed_bproj", "ff_w1", "ff_b1", "ff_w2", "ff_b2",
            "ln1_g", "ln1_b", "ln2_g", "ln2_b", "ln3_g", "ln3_b"]


def kernel(**inputs):
    import numpy as _np
    import concourse.bacc as _bacc
    from concourse import mybir as _mybir
    from concourse.bass_utils import run_bass_kernel_spmd as _run

    maskT = _np.ascontiguousarray(_np.asarray(inputs["mask_BxS_bf0"]).T).view(_np.uint32)
    given = [("x", inputs["x"]), ("ctx", inputs["ctx_1024"]), ("maskT", maskT)]
    given += [(n, inputs["L0_xattn_" + n]) for n in _WEIGHTS]
    nc = _bacc.Bacc("TRN2", target_bir_lowering=False, num_devices=1)
    arrays, args = {}, []
    for name, a in given:
        a = _np.ascontiguousarray(a)
        arrays[f"in_{name}"] = a
        args.append(nc.dram_tensor(f"in_{name}", a.shape, _mybir.dt.from_np(a.dtype), kind="ExternalInput").ap())
    args.append(nc.dram_tensor("out_0", inputs["x"].shape, _mybir.dt.float32, kind="ExternalOutput").ap())
    layer_kernel(nc, *args)
    return _run(nc, [arrays], core_ids=[0]).results[0]["out_0"]
```
